# Optimizing a Trainium2 kernel written in Bass

```python
import numpy as np
import jax
import jax.numpy as jnp

def _softmax(x, axis=-1):
    return jax.nn.softmax(x, axis=axis)
def _gelu(x):
    return jax.nn.gelu(x, approximate=True)
def _silu(x):
    return jax.nn.silu(x)
def _sigmoid(x):
    return jax.nn.sigmoid(x)
def _layernorm(x, axis=-1, eps=1e-5):
    m = jnp.mean(x, axis=axis, keepdims=True)
    v = jnp.var(x, axis=axis, keepdims=True)
    return (x - m) / jnp.sqrt(v + eps)
def _scatter_add(tgt, idx, src, axis=0):
    return tgt.at[idx].add(src)
def _segment_sum(src, seg, n):
    return jax.ops.segment_sum(src, seg, n)

kernel_name = 'mk_conv_preact_d1_conv_nchw64_947ccc'

def setup_inputs(seed: int = 0):
    np.random.seed(seed)
    _w = jnp.asarray
    def _rec_inputs():
        import jax
        import jax.numpy as jnp
        _gk = jax.random.key(seed)
        x = -0.0003929 + 0.9999 * jax.random.normal(jax.random.fold_in(_gk, 1), (16, 64, 128, 128), jnp.float32)
        return x
    x = _rec_inputs()
    def _L0_conv_setup():
        import jax, jax.numpy as jnp
        import numpy as np
        GRID_SIZE = 5
        SPLINE_ORDER = 3
        MODES = 16

        def make_grid():
            h = 2.0 / GRID_SIZE
            return jnp.arange(-SPLINE_ORDER, GRID_SIZE + SPLINE_ORDER + 1, dtype=jnp.float32) * h - 1.0

        def b_splines(x, grid):
            xe = x[..., None]
            bases = ((xe >= grid[:-1]) & (xe < grid[1:])).astype(x.dtype)
            for k in range(1, SPLINE_ORDER + 1):
                left = (xe - grid[:-(k + 1)]) / (grid[k:-1] - grid[:-(k + 1)])
                right = (grid[k + 1:] - xe) / (grid[k + 1:] - grid[1:-k])
                bases = left * bases[..., :-1] + right * bases[..., 1:]
            return bases

        def kan_linear(x, base_w, spline_w, scaler, grid):
            base = jax.nn.silu(x) @ base_w.T
            b = b_splines(x, grid)
            spline = jnp.einsum('nik,oik->no', b, spline_w * scaler[..., None])
            return base + spline

        def spectral_conv2d(x, w1, w2):
            b, c, h, w = x.shape
            x_ft = jnp.fft.rfft2(x)
            out_ft = jnp.zeros((b, c, h, w // 2 + 1), dtype=jnp.complex64)
            out_ft = out_ft.at[:, :, :MODES, :MODES].set(jnp.einsum('bixy,ioxy->boxy', x_ft[:, :, :MODES, :MODES], w1))
            out_ft = out_ft.at[:, :, -MODES:, :MODES].set(jnp.einsum('bixy,ioxy->boxy', x_ft[:, :, -MODES:, :MODES], w2))
            return jnp.fft.irfft2(out_ft, s=(h, w))
        key = jax.random.key(seed)
        ks = jax.random.split(key, 13)
        c = 64
        sc = 1.0 / c
        inp = {'x': jax.random.normal(ks[0], (16, c, 128, 128), dtype=jnp.float32), 'spec_w1_r': jax.random.normal(ks[1], (c, c, MODES, MODES), dtype=jnp.float32) * sc, 'spec_w1_i': jax.random.normal(ks[2], (c, c, MODES, MODES), dtype=jnp.float32) * sc, 'spec_w2_r': jax.random.normal(ks[3], (c, c, MODES, MODES), dtype=jnp.float32) * sc, 'spec_w2_i': jax.random.normal(ks[4], (c, c, MODES, MODES), dtype=jnp.float32) * sc, 'conv_w': jax.random.normal(ks[5], (c, c), dtype=jnp.float32) * 0.05, 'conv_b': jax.random.normal(ks[6], (c,), dtype=jnp.float32) * 0.05, 'k1_base': jax.random.normal(ks[7], (c, c), dtype=jnp.float32) * 0.05, 'k1_spline': jax.random.normal(ks[8], (c, c, GRID_SIZE + SPLINE_ORDER), dtype=jnp.float32) * 0.05, 'k1_scaler': jax.random.normal(ks[9], (c, c), dtype=jnp.float32) * 0.05 + 1.0, 'k2_base': jax.random.normal(ks[10], (c, c), dtype=jnp.float32) * 0.05, 'k2_spline': jax.random.normal(ks[11], (c, c, GRID_SIZE + SPLINE_ORDER), dtype=jnp.float32) * 0.05, 'k2_scaler': jax.random.normal(ks[12], (c, c), dtype=jnp.float32) * 0.05 + 1.0}
        return inp
    _L0_conv_all = _L0_conv_setup()
    _L0_conv_in = {k: v for k, v in _L0_conv_all.items() if k in ('spec_w1_r', 'spec_w1_i', 'spec_w2_r', 'spec_w2_i', 'conv_w', 'conv_b', 'k1_base', 'k1_spline', 'k1_scaler', 'k2_base', 'k2_spline', 'k2_scaler', )}
    del _L0_conv_all

    return {
        "x": x,
        "L0_conv_spec_w1_r": _L0_conv_in["spec_w1_r"],
        "L0_conv_spec_w1_i": _L0_conv_in["spec_w1_i"],
        "L0_conv_spec_w2_r": _L0_conv_in["spec_w2_r"],
        "L0_conv_spec_w2_i": _L0_conv_in["spec_w2_i"],
        "L0_conv_conv_w": _L0_conv_in["conv_w"],
        "L0_conv_conv_b": _L0_conv_in["conv_b"],
        "L0_conv_k1_base": _L0_conv_in["k1_base"],
        "L0_conv_k1_spline": _L0_conv_in["k1_spline"],
        "L0_conv_k1_scaler": _L0_conv_in["k1_scaler"],
        "L0_conv_k2_base": _L0_conv_in["k2_base"],
        "L0_conv_k2_spline": _L0_conv_in["k2_spline"],
        "L0_conv_k2_scaler": _L0_conv_in["k2_scaler"],
    }

def reference(x, L0_conv_spec_w1_r, L0_conv_spec_w1_i, L0_conv_spec_w2_r, L0_conv_spec_w2_i, L0_conv_conv_w, L0_conv_conv_b, L0_conv_k1_base, L0_conv_k1_spline, L0_conv_k1_scaler, L0_conv_k2_base, L0_conv_k2_spline, L0_conv_k2_scaler):
    import jax
    import jax.numpy as jnp
    def _L0_conv_ref(x, spec_w1_r, spec_w1_i, spec_w2_r, spec_w2_i, conv_w, conv_b, k1_base, k1_spline, k1_scaler, k2_base, k2_spline, k2_scaler):
        import jax, jax.numpy as jnp
        import numpy as np
        GRID_SIZE = 5
        SPLINE_ORDER = 3
        MODES = 16

        def make_grid():
            h = 2.0 / GRID_SIZE
            return jnp.arange(-SPLINE_ORDER, GRID_SIZE + SPLINE_ORDER + 1, dtype=jnp.float32) * h - 1.0

        def b_splines(x, grid):
            xe = x[..., None]
            bases = ((xe >= grid[:-1]) & (xe < grid[1:])).astype(x.dtype)
            for k in range(1, SPLINE_ORDER + 1):
                left = (xe - grid[:-(k + 1)]) / (grid[k:-1] - grid[:-(k + 1)])
                right = (grid[k + 1:] - xe) / (grid[k + 1:] - grid[1:-k])
                bases = left * bases[..., :-1] + right * bases[..., 1:]
            return bases

        def kan_linear(x, base_w, spline_w, scaler, grid):
            base = jax.nn.silu(x) @ base_w.T
            b = b_splines(x, grid)
            spline = jnp.einsum('nik,oik->no', b, spline_w * scaler[..., None])
            return base + spline

        def spectral_conv2d(x, w1, w2):
            b, c, h, w = x.shape
            x_ft = jnp.fft.rfft2(x)
            out_ft = jnp.zeros((b, c, h, w // 2 + 1), dtype=jnp.complex64)
            out_ft = out_ft.at[:, :, :MODES, :MODES].set(jnp.einsum('bixy,ioxy->boxy', x_ft[:, :, :MODES, :MODES], w1))
            out_ft = out_ft.at[:, :, -MODES:, :MODES].set(jnp.einsum('bixy,ioxy->boxy', x_ft[:, :, -MODES:, :MODES], w2))
            return jnp.fft.irfft2(out_ft, s=(h, w))
        grid = make_grid()
        w1 = spec_w1_r + 1j * spec_w1_i
        w2 = spec_w2_r + 1j * spec_w2_i
        x1 = spectral_conv2d(x, w1, w2)
        x2 = jnp.einsum('bchw,oc->bohw', x, conv_w) + conv_b[None, :, None, None]
        y = x1 + x2
        b, c, h, w = y.shape
        y_flat = y.transpose(0, 2, 3, 1).reshape(-1, c)
        y_flat = kan_linear(y_flat, k1_base, k1_spline, k1_scaler, grid)
        y_flat = kan_linear(y_flat, k2_base, k2_spline, k2_scaler, grid)
        y = y_flat.reshape(b, h, w, c).transpose(0, 3, 1, 2)
        return jax.nn.gelu(y, approximate=False)

    def _gn(v, G=32, eps=1e-5):
        B_, C_, H_, W_ = v.shape
        g = v.reshape(B_, G, C_ // G, H_, W_)
        m = jnp.mean(g, axis=(2, 3, 4), keepdims=True)
        s = jnp.var(g, axis=(2, 3, 4), keepdims=True)
        return ((g - m) / jnp.sqrt(s + eps)).reshape(v.shape)

    def _ln_c(v, eps=1e-6):
        m = jnp.mean(v, axis=1, keepdims=True)
        s = jnp.var(v, axis=1, keepdims=True)
        return (v - m) / jnp.sqrt(s + eps)

    def _ln_t(v, eps=1e-5):
        m = jnp.mean(v, axis=-1, keepdims=True)
        s = jnp.var(v, axis=-1, keepdims=True)
        return (v - m) / jnp.sqrt(s + eps)

    def _to_tokens(v):
        B_, C_, H_, W_ = v.shape
        return v.reshape(B_, C_, H_ * W_).transpose(0, 2, 1)
    def _from_tokens(t, like):
        B_, C_, H_, W_ = like.shape
        return t.transpose(0, 2, 1).reshape(B_, C_, H_, W_)

    x = x + _L0_conv_ref(_gn(x), L0_conv_spec_w1_r, L0_conv_spec_w1_i, L0_conv_spec_w2_r, L0_conv_spec_w2_i, L0_conv_conv_w, L0_conv_conv_b, L0_conv_k1_base, L0_conv_k1_spline, L0_conv_k1_scaler, L0_conv_k2_base, L0_conv_k2_spline, L0_conv_k2_scaler)
    return x


_drawn_inputs = setup_inputs


def setup_inputs(seed=0):
    import zlib

    import numpy as np

    out = dict(_drawn_inputs(seed))
    spreads = {}
    factors = {'L0_conv_spec_w1_r': 7.278,
     'L0_conv_spec_w1_i': 7.287,
     'L0_conv_spec_w2_r': 7.275,
     'L0_conv_spec_w2_i': 7.292,
     'L0_conv_conv_b': 2.862,
     'L0_conv_k1_scaler': 8.0,
     'L0_conv_k2_scaler': 8.0}
    for name, (base, spread) in spreads.items():
        noise = np.random.default_rng([zlib.crc32(name.encode()), seed]).standard_normal(out[name].shape)
        drawn = base * np.exp(spread * noise) if base else spread * noise
        out[name] = jnp.asarray(drawn.astype(out[name].dtype))
    for name, factor in factors.items():
        out[name] = (out[name] * factor).astype(out[name].dtype)
    return out
```

```python
from contextlib import ExitStack

import numpy as np

import concourse.bass as bass
from concourse import mybir

F32 = mybir.dt.float32
ALU = mybir.AluOpType
ACT = mybir.ActivationFunctionType
AX = mybir.AxisListType

P = 128
B, C, H, W = 16, 64, 128, 128
G = 32
CG = C // G
MODES = 16
EPS = 1e-5
ORDER, GRID = 3, 5
KNOT = 2.0 / GRID
XSCALE = 1.0 / KNOT
XSHIFT = (1.0 + ORDER * KNOT) / KNOT
NB = GRID + ORDER
NF = 1 + NB

NS = MODES + 1
NU = 2 * MODES + 1
CH_GRP = 8
N_GRP = C // CH_GRP
MIX_ROWS = 8
MIX_BUFS = 3
MIX_CHUNKS = 2 * MODES // MIX_ROWS
S_BANK = 8

PAIRS = B // 2
TN = 1024
TH = TN // W
TILES_PAIR = H * W // TN
TILES = PAIRS * TILES_PAIR
MM = 512
RING = 4


def tables():
    h = np.arange(H, dtype=np.float64)
    w = np.arange(W, dtype=np.float64)
    k = np.arange(NS, dtype=np.float64)
    ky = np.arange(MODES, dtype=np.float64)
    ah = 2 * np.pi * np.outer(h, k) / H
    dft_h = np.concatenate([np.cos(ah), np.sin(ah)[:, 1:]], 1)
    aw = 2 * np.pi * np.outer(w, ky) / W
    c, s = np.cos(aw), np.sin(aw)
    dft_w = np.stack([
        np.concatenate([c, -s, c, -s], 1), np.concatenate([-s, -c, s, c], 1),
        np.concatenate([s, c, s, c], 1), np.concatenate([c, -s, -c, s], 1)], 1)
    kx = np.concatenate([np.arange(MODES), np.arange(-MODES, 0)]).astype(np.float64)
    ai = 2 * np.pi * np.outer(kx, h) / H
    inv_h = np.stack([np.stack([np.cos(ai), np.sin(ai)], 1), np.stack([-np.sin(ai), np.cos(ai)], 1)], 1)
    inv_h = inv_h.reshape(4 * MODES, 2, H)
    weight = np.where(ky == 0, 1.0, 2.0)[:, None] / (H * W)
    inv_w = np.concatenate([weight * c.T, -weight * s.T], 0)
    inv_w = np.concatenate([inv_w, inv_w], 0)
    pick = (np.arange(P)[:, None] % C // CG == np.arange(G)[None, :])
    return {n: np.ascontiguousarray(a, dtype=np.float32) for n, a in (
        ("dft_h", dft_h), ("dft_w", dft_w), ("inv_h", inv_h), ("inv_w", inv_w),
        ("pick", pick), ("ident", np.eye(C)))}


def build(nc, x, w1_r, w1_i, w2_r, w2_i, conv_w, conv_b, k1_base, k1_spline, k1_scaler,
          k2_base, k2_spline, k2_scaler, dft_h, dft_w, inv_h, inv_w, pick, ident, out):
    modes_dram = nc.dram_tensor("modes_scratch", [2 * MODES, 2 * B, MODES * C], F32, kind="Internal").ap()
    rows_dram = nc.dram_tensor("rows_scratch", [B, H, 2 * MODES * C], F32, kind="Internal").ap()

    with ExitStack() as keep:
        def held(name, shape):
            return keep.enter_context(nc.sbuf_tensor(name, shape, F32))

        kan_w = [held(f"kan_w{l}", [P, NF, P]) for l in range(2)]
        conv_blk = held("conv_blk", [P, P])
        conv_bias = held("conv_bias", [P, 1])
        inv_w_sb = held("inv_w_sb", [P // 2, W])
        pair_rs = held("pair_rs", [P, PAIRS])
        pair_consts = held("pair_consts", [P, PAIRS, 3])
        first_half(nc, locals())
        second_half(nc, x, out, rows_dram, kan_w, conv_blk, inv_w_sb, pair_consts)


def first_half(nc, t):
    with ExitStack() as ctx:
        def sb(name, shape):
            return ctx.enter_context(nc.sbuf_tensor(name, shape, F32))

        modes = sb("modes", [P, NS, 2, 2 * MODES, B])
        stats = sb("stats", [P, B, G, 6])
        t = dict(t, modes=modes, stats=stats)
        prepare_weights(nc, t)
        forward(nc, t)
        with ExitStack() as inner:
            t["rs_c"] = inner.enter_context(nc.sbuf_tensor("rs_c", [P, B], F32))
            t["mix_w"] = [inner.enter_context(nc.sbuf_tensor(f"mix_w{i}", [P, C, MIX_ROWS, MODES], F32))
                          for i in range(MIX_BUFS)]
            t["mix_loaded"] = [inner.enter_context(nc.semaphore(f"mix_loaded{i}")) for i in range(MIX_BUFS)]
            statistics(nc, t)
            mix_modes(nc, t)
    inverse_rows(nc, t)


def load_mix_chunk(nc, t, k):
    half, rows = k // (MODES // MIX_ROWS), k % (MODES // MIX_ROWS) * MIX_ROWS
    for part, src in enumerate(((t["w1_r"], t["w1_i"]), (t["w2_r"], t["w2_i"]))[half]):
        nc.sync.dma_start(t["mix_w"][k % MIX_BUFS][part * C:(part + 1) * C],
                          src[:, :, rows:rows + MIX_ROWS, :]).then_inc(t["mix_loaded"][k % MIX_BUFS], 16)


def prepare_weights(nc, t):
    conv_blk, conv_bias, kan_w, inv_w_sb = t["conv_blk"], t["conv_bias"], t["kan_w"], t["inv_w_sb"]
    with ExitStack() as ctx:
        def sb(name, shape):
            return ctx.enter_context(nc.sbuf_tensor(name, shape, F32))

        def sem(name):
            return ctx.enter_context(nc.semaphore(name))

        spline = [sb(f"spline{l}", [C, C, NB]) for l in range(2)]
        scaler = [sb(f"scaler{l}", [C, C]) for l in range(2)]
        mats = [sb(f"mats{l}", [C, NF, 2, C]) for l in range(2)]
        conv_nat = sb("conv_nat", [C, 2, C])
        eye = sb("eye", [C, C])
        turned = [ctx.enter_context(nc.psum_tensor(f"turned{i}", [P, C], F32)) for i in range(2)]
        natural_loaded, consts_loaded = sem("natural_loaded"), sem("consts_loaded")
        scaled, sixth, mixed, cleared = sem("scaled"), sem("sixth"), sem("mixed"), sem("cleared")
        turn_done, turn_kept = sem("turn_done"), sem("turn_kept")
        n_natural = 0
        jobs = [(l, f) for l in range(2) for f in range(NF)] + [(None, 0)]

        block = ctx.enter_context(nc.Block())

        @block.sync
        def _(sp):
            loads = [(eye[:], t["ident"])]
            for l, (b_, s_, c_) in enumerate(((t["k1_base"], t["k1_spline"], t["k1_scaler"]),
                                              (t["k2_base"], t["k2_spline"], t["k2_scaler"]))):
                loads += [(spline[l][:], s_), (scaler[l][:], c_)]
                loads += [(mats[l][:, 0, d, :], b_) for d in range(2)]
            loads += [(conv_nat[:, d, :], t["conv_w"]) for d in range(2)]
            for dst, src in loads:
                sp.dma_start(dst, src).then_inc(natural_loaded, 16)
            for d in range(2):
                sp.dma_start(conv_bias[d * C:(d + 1) * C, :],
                             t["conv_b"].rearrange("(c a) -> c a", a=1)).then_inc(consts_loaded, 16)
            sp.dma_start(inv_w_sb[:], t["inv_w"]).then_inc(consts_loaded, 16)
            sp.wait_ge(natural_loaded, 16 * len(loads))
            sp.wait_ge(consts_loaded, 48)

        n_loads = 1 + 2 * 4 + 2

        @block.vector
        def _(dve):
            nc.vector.memset(kan_w[0][:], 0.0).then_inc(cleared, 1)
            nc.vector.memset(kan_w[1][:], 0.0).then_inc(cleared, 1)
            nc.vector.memset(conv_blk[:], 0.0).then_inc(cleared, 1)
            dve.wait_ge(natural_loaded, 16 * n_loads)
            for l in range(2):
                nc.vector.scalar_tensor_tensor(
                    out=spline[l][:], in0=spline[l][:], scalar=1.0 / 6.0,
                    in1=scaler[l][:].unsqueeze(2).to_broadcast([C, C, NB]),
                    op0=ALU.mult, op1=ALU.mult).then_inc(scaled, 1)
            for l in range(2):
                dve.wait_ge(scaled, l + 1)
                w = [spline[l][:, :, k] for k in range(NB)]
                for rho in range(2):
                    f = 1 + 4 * rho
                    for d in range(2):
                        m = mats[l][:, :, d, :]
                        nc.vector.tensor_tensor(m[:, f, :], w[rho + 4], w[rho], ALU.subtract).then_inc(mixed, 1)
                        nc.vector.tensor_scalar(m[:, f + 1, :], w[rho + 4], -1.0, None, ALU.mult).then_inc(mixed, 1)
                        nc.vector.tensor_copy(m[:, f + 2, :], w[rho + 2]).then_inc(mixed, 1)
                        nc.vector.tensor_tensor(m[:, f + 3, :], w[rho + 6], w[rho + 2], ALU.subtract).then_inc(mixed, 1)
            dve.wait_ge(cleared, 3)
            for n, (l, f) in enumerate(jobs):
                dst = conv_blk[:] if l is None else kan_w[l][:, f, :]
                dve.wait_ge(turn_done, n + 1)
                nc.vector.tensor_copy(dst[0:C, 0:C], turned[n % 2][0:C, :])
                nc.vector.tensor_copy(dst[C:P, C:P], turned[n % 2][C:P, :]).then_inc(turn_kept, 1)

        @block.tensor
        def _(pe):
            pe.wait_ge(natural_loaded, 16 * n_loads)
            pe.wait_ge(mixed, 2 * 2 * 2 * 4)
            for n, (l, f) in enumerate(jobs):
                src = conv_nat[:] if l is None else mats[l][:, f, :, :]
                if n >= 2:
                    pe.wait_ge(turn_kept, n - 1)
                nc.tensor.matmul(turned[n % 2][:], src.rearrange("o d i -> o (d i)"), eye[:],
                                 start=True, stop=True).then_inc(turn_done, 1)


def forward(nc, t):
    modes, stats = t["modes"], t["stats"]
    with ExitStack() as ctx:
        def sb(name, shape):
            return ctx.enter_context(nc.sbuf_tensor(name, shape, F32))

        def sem(name):
            return ctx.enter_context(nc.semaphore(name))

        PARTS = 8
        QC = C // PARTS
        img = sb("img", [P, 2, C, W])
        freq = sb("freq", [P, 2, NU, C])
        dft_h_sb = sb("dft_h_sb", [P, NU])
        dft_w_sb = sb("dft_w_sb", [P, 4, 4 * MODES])
        along_h = [ctx.enter_context(nc.psum_tensor(f"along_h{i}", [P, CH_GRP, NU], F32)) for i in range(4)]
        along_w = [ctx.enter_context(nc.psum_tensor(f"along_w{i}", [P, S_BANK, 2, 2 * MODES], F32)) for i in range(3)]
        img_loaded = [[sem(f"img_loaded{p}{q}") for q in range(PARTS)] for p in range(2)]
        tables_loaded = sem("tables_loaded")
        along_h_done = sem("along_h_done")
        freq_ready = sem("freq_ready")
        along_w_done = sem("along_w_done")
        modes_kept = sem("modes_kept")

        block = ctx.enter_context(nc.Block())

        @block.sync
        def _(sp):
            def load(par, b):
                for q in range(PARTS):
                    src = t["x"][b].rearrange("c h w -> h c w") if isinstance(b, int) else \
                        t["x"][bass.ds(b, 1)].rearrange("a c h w -> h (a c) w")
                    sp.dma_start(img[:, par, q * QC:(q + 1) * QC, :],
                                 src[:, q * QC:(q + 1) * QC, :]).then_inc(img_loaded[par][q], 16)

            sp.dma_start(dft_h_sb[:], t["dft_h"]).then_inc(tables_loaded, 16)
            sp.dma_start(dft_w_sb[:], t["dft_w"]).then_inc(tables_loaded, 16)
            load(0, 0)
            load(1, 1)
            with sp.Fori(1, B // 2) as b2:
                for par in range(2):
                    sp.wait_ge(modes_kept, 2 * b2 + par)
                    load(par, 2 * b2 + par)

        @block.vector
        def _(dve):
            with dve.Fori(0, B // 2) as b2:
                for par in range(2):
                    b = 2 * b2 + par
                    for q in range(PARTS):
                        dve.wait_ge(img_loaded[par][q], 16 * (b2 + 1))
                        for g in range(q * QC // CG, (q + 1) * QC // CG):
                            ins = nc.vector.bn_stats(stats[:, bass.ds(b, 1), g, :],
                                                     img[:, par, CG * g:CG * (g + 1), :].rearrange("p c w -> p (c w)"))
                    dve.wait_ge(along_w_done, b + 1)
                    for i in range(3):
                        n = min(S_BANK, NS - S_BANK * i)
                        ins = nc.vector.tensor_copy(
                            modes[:, S_BANK * i:S_BANK * i + n, :, :, bass.ds(b, 1)].rearrange("p s g m b -> p (s g m) b"),
                            along_w[i][:, 0:n, :, :].rearrange("p s g (m b) -> p (s g m) b", b=1))
                    ins.then_inc(modes_kept, 1)

        @block.tensor
        def _(pe):
            pe.sem_inc(modes_kept, 1)
            pe.wait_ge(tables_loaded, 32)
            with pe.Fori(0, B // 2) as b2:
                for par in range(2):
                    b = 2 * b2 + par
                    for g in range(N_GRP):
                        if g % (QC // CH_GRP) == 0:
                            pe.wait_ge(img_loaded[par][g * CH_GRP // QC], 16 * (b2 + 1))
                        pe.wait_ge(freq_ready, N_GRP * b + (g + 1))
                        for c in range(CH_GRP):
                            ins = nc.tensor.matmul(along_h[g % 4][:, c, :], img[:, par, CH_GRP * g + c, :],
                                                   dft_h_sb[:], start=True, stop=True)
                        ins.then_inc(along_h_done, 1)
                    pe.wait_ge(freq_ready, N_GRP * b + (N_GRP + 4))
                    pe.wait_ge(modes_kept, b + 1)
                    for s in range(NS):
                        for high in range(2):
                            dst = along_w[s // S_BANK][high * C:(high + 1) * C, s % S_BANK, :, :]
                            dst = dst.rearrange("p g m -> p (g m)")
                            ins = nc.tensor.matmul(dst, freq[:, par, s, :], dft_w_sb[:, 2 * high, :],
                                                   start=True, stop=(s == 0))
                            if s > 0:
                                ins = nc.tensor.matmul(dst, freq[:, par, MODES + s, :], dft_w_sb[:, 2 * high + 1, :],
                                                       start=False, stop=True)
                    ins.then_inc(along_w_done, 1)

        @block.scalar
        def _(act):
            act.sem_inc(freq_ready, 4)
            with act.Fori(0, B // 2) as b2:
                for par in range(2):
                    b = 2 * b2 + par
                    for g in range(N_GRP):
                        act.wait_ge(along_h_done, N_GRP * b + (g + 1))
                        nc.scalar.activation(freq[:, par, :, CH_GRP * g:CH_GRP * (g + 1)],
                                             along_h[g % 4][:].rearrange("p c u -> p u c"),
                                             ACT.Copy).then_inc(freq_ready, 1)


def statistics(nc, t):
    modes, stats = t["modes"], t["stats"]
    conv_blk, conv_bias, pair_rs, pair_consts = t["conv_blk"], t["conv_bias"], t["pair_rs"], t["pair_consts"]
    with ExitStack() as ctx:
        def sb(name, shape):
            return ctx.enter_context(nc.sbuf_tensor(name, shape, F32))

        def sem(name):
            return ctx.enter_context(nc.semaphore(name))

        mean_all = sb("mean_all", [P, 1])
        avg = sb("avg", [P, P])
        avg_sq = sb("avg_sq", [P, P])
        pick_sb = sb("pick_sb", [P, G])
        mean_bg = sb("mean_bg", [P, B, G])
        dev = sb("dev", [P, 2, B, G])
        dev_sq = sb("dev_sq", [P, 2, B, G])
        var = sb("var", [P, B, G])
        root = sb("root", [P, B, G])
        quot = sb("quot", [P, B, G])
        rs_bg = sb("rs_bg", [P, B, G])
        tmp = sb("tmp", [P, B, G])
        rs_c = t["rs_c"]
        mean_c = sb("mean_c", [P, B])
        pair_rm = sb("pair_rm", [P, PAIRS])
        pair_mean = sb("pair_mean", [P, PAIRS])
        ps_mean = ctx.enter_context(nc.psum_tensor("ps_mean", [P, B, G], F32))
        ps_var = ctx.enter_context(nc.psum_tensor("ps_var", [P, B, G], F32))
        ps_bias = ctx.enter_context(nc.psum_tensor("ps_bias", [P, PAIRS], F32))
        pick_loaded, set_up = sem("pick_loaded"), sem("set_up")
        mean_done, dev_ready, var_done = sem("mean_done"), sem("dev_ready"), sem("var_done")
        var_ready, root_ready, chain = sem("var_ready"), sem("root_ready"), sem("chain")
        rm_ready, bias_done = sem("rm_ready"), sem("bias_done")
        block = ctx.enter_context(nc.Block())

        @block.sync
        def _(sp):
            sp.dma_start(pick_sb[:], t["pick"]).then_inc(pick_loaded, 16)
            for k in range(MIX_BUFS):
                load_mix_chunk(nc, t, k)

        @block.tensor
        def _(pe):
            pe.wait_ge(set_up, 2)
            for eo in range(2):
                ins = nc.tensor.matmul(ps_mean[:], avg[:], stats[:, :, :, 3 * eo + 1], start=(eo == 0), stop=(eo == 1))
            ins.then_inc(mean_done, 1)
            pe.wait_ge(dev_ready, 1)
            for eo in range(2):
                nc.tensor.matmul(ps_var[:], avg_sq[:], stats[:, :, :, 3 * eo + 2], start=(eo == 0), stop=False)
            for eo in range(2):
                ins = nc.tensor.matmul(ps_var[:], avg_sq[:], dev_sq[:, eo], start=False, stop=(eo == 1))
            ins.then_inc(var_done, 1)
            pe.wait_ge(rm_ready, 1)
            nc.tensor.matmul(ps_bias[:], conv_blk[:], pair_rm[:], start=True, stop=True).then_inc(bias_done, 1)

        @block.scalar
        def _(act):
            act.wait_ge(var_ready, 1)
            nc.scalar.activation(root[:], var[:], ACT.Sqrt).then_inc(root_ready, 1)

        @block.vector
        def _(dve):
            links = [0]

            def link(ins):
                links[0] += 1
                ins.then_inc(chain, 1)
                dve.wait_ge(chain, links[0])

            nc.vector.memset(avg[:], 0.5 / P).then_inc(set_up, 1)
            nc.vector.memset(avg_sq[:], 1.0 / (CG * H * W)).then_inc(set_up, 1)
            dve.wait_ge(mean_done, 1)
            link(nc.vector.tensor_copy(mean_bg[:], ps_mean[:]))
            for eo in range(2):
                link(nc.vector.tensor_tensor(dev[:, eo], stats[:, :, :, 3 * eo + 1], mean_bg[:], ALU.subtract))
            n_half = CG * W // 2
            nc.vector.scalar_tensor_tensor(out=dev_sq[:], in0=dev[:], scalar=float(n_half), in1=dev[:],
                                           op0=ALU.mult, op1=ALU.mult).then_inc(dev_ready, 1)
            dve.wait_ge(var_done, 1)
            link(nc.vector.tensor_scalar(var[:], ps_var[:], EPS, None, ALU.add))
            dve.sem_inc(var_ready, 1)
            dve.wait_ge(root_ready, 1)
            link(nc.vector.reciprocal(quot[:], root[:]))
            link(nc.vector.tensor_tensor(tmp[:], quot[:], var[:], ALU.mult))
            link(nc.vector.tensor_tensor(quot[:], tmp[:], root[:], ALU.add))
            link(nc.vector.tensor_scalar(tmp[:], quot[:], 0.5, None, ALU.mult))
            link(nc.vector.reciprocal(rs_bg[:], tmp[:]))
            dve.wait_ge(pick_loaded, 16)
            for src, dst in ((rs_bg, rs_c), (mean_bg, mean_c)):
                link(nc.vector.tensor_tensor(tmp[:], src[:], pick_sb[:].unsqueeze(1).to_broadcast([P, B, G]), ALU.mult))
                link(nc.vector.tensor_reduce(dst[:], tmp[:], AX.X, ALU.add))
            for half in range(2):
                rows = slice(half * C, (half + 1) * C)
                link(nc.vector.tensor_copy(pair_rs[rows, :], rs_c[rows, half:B:2]))
                link(nc.vector.tensor_copy(pair_mean[rows, :], mean_c[rows, half:B:2]))
            nc.vector.tensor_tensor(pair_rm[:], pair_rs[:], pair_mean[:], ALU.mult).then_inc(rm_ready, 1)
            dve.wait_ge(bias_done, 1)
            link(nc.vector.tensor_copy(pair_consts[:, :, 0], pair_rs[:]))
            link(nc.vector.tensor_scalar(pair_consts[:, :, 1], ps_bias[:], -1.0, conv_bias[:, 0:1], ALU.mult, ALU.add))
            link(nc.vector.tensor_scalar(pair_consts[:, :, 2], pair_consts[:, :, 1], XSCALE, XSHIFT, ALU.mult, ALU.add))
            for half in range(2):
                rows = slice(half * C, (half + 1) * C)
                dc = modes[rows, 0, 0, half * MODES, :]
                link(nc.vector.scalar_tensor_tensor(out=dc, in0=mean_c[rows, :], scalar=-float(H * W), in1=dc,
                                                    op0=ALU.mult, op1=ALU.add))


def mix_modes(nc, t):
    modes, modes_dram, rs_c = t["modes"], t["modes_dram"], t["rs_c"]
    with ExitStack() as ctx:
        def sb(name, shape):
            return ctx.enter_context(nc.sbuf_tensor(name, shape, F32))

        def sem(name):
            return ctx.enter_context(nc.semaphore(name))

        normed = [sb(f"normed{i}", [P, MODES + 1, 2, B]) for i in range(2)]
        mixed = [sb(f"mixed{i}", [2 * B, MODES * C]) for i in range(2)]
        ps = [ctx.enter_context(nc.psum_tensor(f"mix_ps{i}", [C, 2, MM], F32)) for i in range(2)]
        cleared = sem("mix_cleared")
        normed_ready, mix_done, mix_kept = sem("normed_ready"), sem("mix_done"), sem("mix_kept")
        stored = [sem(f"mix_stored{i}") for i in range(2)]
        block = ctx.enter_context(nc.Block())
        CHUNK = MIX_ROWS // 2

        @block.vector
        def _(dve):
            nc.vector.memset(normed[0][:, MODES, :, :], 0.0).then_inc(cleared, 1)
            nc.vector.memset(normed[1][:, MODES, :, :], 0.0).then_inc(cleared, 1)
            for half in range(2):
                with dve.Fori(0, MODES // 2) as x2:
                    for u in range(2):
                        xx = 2 * x2 + u
                        s = xx if half == 0 else xx * -1 + MODES
                        dve.wait_ge(mix_done, xx + (MODES * half + 1))
                        nc.vector.tensor_tensor(
                            normed[u][:, 0:MODES, :, :].rearrange("p k r b -> p r k b"),
                            modes[:, bass.ds(s, 1), half, :, :].rearrange("p s (r k) b -> p (s r) k b", r=2),
                            rs_c[:].unsqueeze(1).unsqueeze(1).to_broadcast([P, 2, MODES, B]),
                            ALU.mult).then_inc(normed_ready, 1)

        @block.tensor
        def _(pe):
            pe.sem_inc(mix_done, 2)
            pe.wait_ge(cleared, 2)
            for k in range(MIX_CHUNKS):
                pe.wait_ge(t["mix_loaded"][k % MIX_BUFS], 32 * (k // MIX_BUFS + 1))
                with pe.Fori(0, CHUNK) as x2:
                    for u in range(2):
                        row = 2 * x2 + u
                        pe.wait_ge(normed_ready, row + (MIX_ROWS * k + 1))
                        pe.wait_ge(mix_kept, row + (MIX_ROWS * k + 1))
                        for ky in range(MODES):
                            ins = nc.tensor.matmul(
                                ps[u][:, ky // 8, (ky % 8) * C:(ky % 8 + 1) * C],
                                normed[u][:, ky:ky + 2, :, :].rearrange("p k r b -> p (k r b)"),
                                t["mix_w"][k % MIX_BUFS][:, :, bass.ds(row, 1), ky].rearrange("p o x -> p (o x)"),
                                start=True, stop=True)
                        ins.then_inc(mix_done, 1)

        @block.scalar
        def _(act):
            act.sem_inc(mix_kept, 2)
            act.sem_inc(stored[0], 16)
            act.sem_inc(stored[1], 16)
            with act.Fori(0, MODES) as x2:
                for u in range(2):
                    act.wait_ge(mix_done, 2 * x2 + (u + 3))
                    act.wait_ge(stored[u], 16 * (x2 + 1))
                    nc.scalar.activation(mixed[u][:], ps[u][0:2 * B, :, :].rearrange("p a n -> p (a n)"),
                                         ACT.Copy).then_inc(mix_kept, 1)

        @block.sync
        def _(sp):
            for k in range(MIX_CHUNKS):
                if k + MIX_BUFS - 1 >= MIX_BUFS and k + MIX_BUFS - 1 < MIX_CHUNKS:
                    sp.wait_ge(mix_done, MIX_ROWS * k + 2)
                    load_mix_chunk(nc, t, k + MIX_BUFS - 1)
                with sp.Fori(0, CHUNK) as x2:
                    for u in range(2):
                        n = 2 * x2 + (u + MIX_ROWS * k)
                        sp.wait_ge(mix_kept, n + 3)
                        sp.dma_start(modes_dram[bass.ds(n, 1)].rearrange("a q f -> (a q) f"),
                                     mixed[u][:]).then_inc(stored[u], 16)
            for u in range(2):
                sp.wait_ge(stored[u], 16 * (MODES + 1))


def inverse_rows(nc, t):
    modes_dram, rows_dram = t["modes_dram"], t["rows_dram"]
    with ExitStack() as ctx:
        def sb(name, shape):
            return ctx.enter_context(nc.sbuf_tensor(name, shape, F32))

        def sem(name):
            return ctx.enter_context(nc.semaphore(name))

        inv_h_sb = sb("inv_h_sb", [4 * MODES, 2, H])
        spec = [sb(f"spec{i}", [4 * MODES, MODES * C]) for i in range(2)]
        rows = [sb(f"rows{i}", [H, 2 * MODES * C]) for i in range(2)]
        ps = [ctx.enter_context(nc.psum_tensor(f"rows_ps{i}", [H, MM], F32)) for i in range(4)]
        inv_h_loaded = sem("inv_h_loaded")
        spec_loaded = [sem(f"spec_loaded{i}") for i in range(2)]
        rows_done, rows_kept = sem("rows_done"), sem("rows_kept")
        rows_stored = [sem(f"rows_stored{i}") for i in range(2)]
        src = modes_dram.rearrange("k (q b) f -> (k q) b f", b=B)
        block = ctx.enter_context(nc.Block())

        @block.sync
        def _(sp):
            sp.dma_start(inv_h_sb[:], t["inv_h"]).then_inc(inv_h_loaded, 16)
            for u in range(2):
                sp.dma_start(spec[u][:], src[:, u, :]).then_inc(spec_loaded[u], 16)
            with sp.Fori(0, B // 2 - 1) as b2:
                for u in range(2):
                    b = 2 * b2 + u
                    sp.wait_ge(rows_kept, 4 * b + 8)
                    sp.dma_start(rows_dram[bass.ds(b, 1)].rearrange("a h f -> (a h) f"),
                                 rows[u][:]).then_inc(rows_stored[u], 16)
                    sp.dma_start(spec[u][:], src[:, bass.ds(b + 2, 1), :].rearrange("k b f -> k (b f)"))\
                      .then_inc(spec_loaded[u], 16)
            for u in range(2):
                b = B - 2 + u
                sp.wait_ge(rows_kept, 4 * b + 8)
                sp.dma_start(rows_dram[b], rows[u][:]).then_inc(rows_stored[u], 16)
            for u in range(2):
                sp.wait_ge(rows_stored[u], 16 * (B // 2 + 1))

        @block.tensor
        def _(pe):
            pe.wait_ge(inv_h_loaded, 16)
            with pe.Fori(0, B // 2) as b2:
                for u in range(2):
                    b = 2 * b2 + u
                    pe.wait_ge(spec_loaded[u], 16 * (b2 + 1))
                    for k in range(4):
                        pe.wait_ge(rows_kept, 4 * b + (k + 1))
                        nc.tensor.matmul(ps[k][:], inv_h_sb[:, k // 2, :], spec[u][:, (k % 2) * MM:(k % 2 + 1) * MM],
                                         start=True, stop=True).then_inc(rows_done, 1)

        @block.scalar
        def _(act):
            act.sem_inc(rows_kept, 4)
            act.sem_inc(rows_stored[0], 16)
            act.sem_inc(rows_stored[1], 16)
            with act.Fori(0, B // 2) as b2:
                for u in range(2):
                    b = 2 * b2 + u
                    act.wait_ge(rows_stored[u], 16 * (b2 + 1))
                    for k in range(4):
                        act.wait_ge(rows_done, 4 * b + (k + 1))
                        nc.scalar.activation(rows[u][:, k * MM:(k + 1) * MM], ps[k][:], ACT.Copy).then_inc(rows_kept, 1)


def second_half(nc, x, out, rows_dram, kan_w, conv_blk, inv_w_sb, pair_consts):
    with ExitStack() as ctx:
        def sb(name, shape):
            return ctx.enter_context(nc.sbuf_tensor(name, shape, F32))

        def ps(name):
            return ctx.enter_context(nc.psum_tensor(name, [P, TN], F32))

        def sem(name):
            return ctx.enter_context(nc.semaphore(name))

        x_ring = sb("x_ring", [P, RING, TN])
        rows = sb("rows_t", [P // 2, 2, TH, P])
        consts = sb("consts", [P, 3])
        conv_t = sb("conv_t", [P, P])
        X = [[sb(f"X{l}{p}", [P, TN]) for p in range(2)] for l in range(2)]
        S = [[sb(f"S{l}{p}", [P, TN]) for p in range(2)] for l in range(2)]
        fold = [sb(f"fold{p}", [P, TN]) for p in range(2)]
        e_ = [sb(f"e{p}", [P, TN]) for p in range(2)]
        g_ = [sb(f"g{p}", [P, TN]) for p in range(2)]
        q_ = [sb(f"q{p}", [P, TN]) for p in range(2)]
        F1, F2, Cn, Cp = sb("F1", [P, TN]), sb("F2", [P, TN]), sb("Cn", [P, TN]), sb("Cp", [P, TN])
        phi = [[sb(f"phi{p}{m}", [P, TN]) for m in range(4)] for p in range(2)]
        act_out = sb("act_out", [P, TN])
        const = {v: sb(f"const{v}".replace("-", "m"), [P, 1]) for v in (-1, -2, -4, -7, 10)}
        xshift = sb("xshift", [P, 1])
        y_ps, l2_ps = ps("y_ps"), ps("l2_ps")
        l1_ps = [ps("l1_ps0"), ps("l1_ps1")]

        x_loaded, rows_loaded, rows_zero, out_stored = sem("x_loaded"), sem("rows_loaded"), sem("rows_zero"), sem("out_stored")
        consts_ready, conv_ready = sem("consts_ready"), sem("conv_ready")
        y_done = sem("y_done")
        X_ready = [sem("X0_ready"), sem("X1_ready")]
        S_ready = [sem("S0_ready"), sem("S1_ready")]
        shifts_ready = sem("shifts_ready")
        gelu_ready = sem("gelu_ready")
        x_added = sem("x_added")
        clip_ready = sem("clip_ready")
        clip0_ready = sem("clip0_ready")
        fold_ready = sem("fold_ready")
        zigzag_ready = sem("zigzag_ready")
        F_ready, C_ready = sem("F_ready"), sem("C_ready")
        phi_ready = sem("phi_ready")
        phi_used = sem("phi_used")

        first, last = -1, TILES - 1
        LOOP0, LOOP1 = 2, TILES - 4
        assert (LOOP1 - LOOP0) % 2 == 0

        def steps(eng, body):
            for i in range(first, LOOP0):
                body(i, i)
            with eng.Fori(0, (LOOP1 - LOOP0) // 2) as turn:
                for u in range(2):
                    body(2 * turn + (LOOP0 + u), LOOP0 + u)
            for i in range(LOOP1, last + 1):
                body(i, i)

        def l1_over(j):
            return 2 if isinstance(j, int) and j == 0 else 4 * j

        def l2_over(j):
            return 4 * TILES if isinstance(j, int) and j == last else 4 * j + 6

        def has_l1(like):
            return like + 1 <= last

        def has_l2(like):
            return like >= 0

        def halves(i, like):
            found = []
            m = 2 * i + 1 if like >= 0 else 0
            if has_l1(like):
                found += [(m, 0, i + 1, (like + 1) % 2, rho) for rho in range(2)]
                m = m + 1
            if has_l2(like):
                found += [(m, 1, i, like % 2, rho) for rho in range(2)]
            return found

        def next_but_one(i, like):
            return (halves(i, like) + (halves(i + 1, like + 1) if like < last else []))[2:]

        def tile_of(ring, j):
            slot = j % RING if isinstance(j, int) else j & (RING - 1)
            return ring[:, slot, :] if isinstance(slot, int) else ring[:, bass.ds(slot, 1), :].rearrange("p a n -> p (a n)")

        block = ctx.enter_context(nc.Block())

        @block.sync
        def _(sp):
            def place(j):
                if isinstance(j, int):
                    return j // TILES_PAIR, j % TILES_PAIR, j % RING, j % 2
                return (j >> 4) & (PAIRS - 1), j & (TILES_PAIR - 1), j & (RING - 1), j & 1

            def dram(a, pair, k):
                v = a.rearrange("(p i) c (t h) w -> p (i c) t (h w)", i=2, h=TH)
                return v[bass.ds(pair, 1), :, bass.ds(k, 1), :].rearrange("p c t n -> (p c) (t n)")

            def load(where):
                pair, k, slot, par = where
                sp.dma_start(x_ring[:, bass.ds(slot, 1), :].rearrange("p a n -> p (a n)"),
                             dram(x, pair, k)).then_inc(x_loaded, 16)
                for i in range(2):
                    src = rows_dram.rearrange("(p i) (t h) (q o) -> p i t q h o", i=2, h=TH, o=C)
                    src = src[bass.ds(pair, 1), i, bass.ds(k, 1), :, :, :].rearrange("p t q h o -> (p t q) h o")
                    dst = rows[i * 2 * MODES:(i + 1) * 2 * MODES, bass.ds(par, 1), :, i * C:(i + 1) * C]
                    sp.dma_start(dst.rearrange("q a h o -> q (a h) o"), src).then_inc(rows_loaded, 16)

            def store(where):
                sp.dma_start(dram(out, *where[:2]), act_out[:]).then_inc(out_stored, 16)

            sp.wait_ge(rows_zero, 1)
            load(place(0))
            sp.wait_ge(x_loaded, 16)
            sp.wait_ge(rows_loaded, 32)
            load(place(1))
            for j in range(2, RING):
                sp.wait_ge(y_done, j)
                load(place(j))
            with sp.Fori(1, TILES - RING + 1) as i:
                stored, loaded = place(i - 1), place(i + (RING - 1))
                sp.wait_ge(x_added, 16 * i)
                store(stored)
                load(loaded)
            for j in range(TILES - RING, TILES):
                sp.wait_ge(x_added, 16 * (j + 1))
                store(place(j))
            sp.wait_ge(out_stored, 16 * TILES)

        @block.gpsimd
        def _(pool):
            with pool.Fori(0, TILES) as j:
                pool.wait_ge(gelu_ready, j + 1)
                pool.dma_start(act_out[:], tile_of(x_ring, j), accum_op=ALU.add).then_inc(x_added, 16)

        @block.vector
        def _(dve):
            def prepare(j):
                if not isinstance(j, int) or j > 0:
                    dve.wait_ge(S_ready[0], j)
                pair = j // TILES_PAIR if isinstance(j, int) else (j >> 4) & (PAIRS - 1)
                nc.vector.tensor_copy(consts[:], pair_consts[:, bass.ds(pair, 1), :].rearrange("p a k -> p (a k)"))\
                    .then_inc(consts_ready, 1)
                dve.wait_ge(consts_ready, j + 1)
                nc.vector.tensor_scalar(conv_t[:], conv_blk[:], consts[:, 0:1], None, ALU.mult).then_inc(conv_ready, 1)

            def clip(half):
                m, layer, tile, par, rho = half
                if rho == 0:
                    return
                dve.wait_ge(X_ready[layer], tile + 1)
                nc.vector.tensor_scalar(fold[rho][:], X[layer][par][:], float(rho), float(rho + 10),
                                        ALU.max, ALU.min).then_inc(clip_ready, 1)

            def features(half, like):
                turn, layer, tile, par, rho = half
                n = 2 * turn + rho
                x_ = X[layer][par]
                dve.wait_ge(zigzag_ready, 3 * n + 3)
                nc.vector.scalar_tensor_tensor(out=F1[:], in0=q_[rho][:], scalar=3.0, in1=e_[rho][:],
                                               op0=ALU.subtract, op1=ALU.mult).then_inc(F_ready, 1)
                nc.vector.scalar_tensor_tensor(out=F2[:], in0=g_[rho][:], scalar=3.0, in1=q_[rho][:],
                                               op0=ALU.subtract, op1=ALU.mult).then_inc(F_ready, 1)
                dve.wait_ge(F_ready, 2 * n + 2)
                nc.vector.scalar_tensor_tensor(out=Cn[:], in0=F1[:], scalar=1.0, in1=F2[:],
                                               op0=ALU.subtract, op1=ALU.add).then_inc(C_ready, 1)
                nc.vector.scalar_tensor_tensor(out=Cp[:], in0=F1[:], scalar=1.0, in1=F2[:],
                                               op0=ALU.add, op1=ALU.subtract).then_inc(C_ready, 1)
                if like >= 0:
                    dve.wait_ge(phi_used, n - 1)
                for m, (knot, op, src) in enumerate(((4, ALU.is_lt, Cn), (8, ALU.is_lt, Cn),
                                                     (2, ALU.is_ge, Cp), (6, ALU.is_ge, Cp))):
                    dve.wait_ge(C_ready, 2 * n + 1 + m // 2)
                    nc.vector.scalar_tensor_tensor(out=phi[rho][m][:], in0=x_[:], scalar=float(rho + knot),
                                                   in1=src[:], op0=op, op1=ALU.mult).then_inc(phi_ready, 1)

            def step(i, like):
                after = next_but_one(i, like)
                for k, half in enumerate(halves(i, like)):
                    features(half, like)
                    if k < len(after):
                        clip(after[k])
                if 0 <= like and like + 3 <= last:
                    prepare(i + 3)

            nc.vector.memset(rows[:], 0.0).then_inc(rows_zero, 1)
            for v, tile in const.items():
                nc.vector.memset(tile[:], float(v)).then_inc(shifts_ready, 1)
            nc.vector.memset(xshift[:], XSHIFT).then_inc(shifts_ready, 1)
            for j in range(3):
                prepare(j)
            for half in halves(first, first):
                clip(half)
            steps(dve, step)

        @block.scalar
        def _(act):
            def evacuate_y(j, par, like):
                act.wait_ge(y_done, j + 1)
                act.wait_ge(consts_ready, j + 1)
                if like >= 0:
                    act.wait_ge(phi_used, l1_over(j - 2))
                nc.scalar.activation(X[0][par][:], y_ps[:], ACT.Relu, bias=consts[:, 2:3],
                                     scale=XSCALE).then_inc(X_ready[0], 1)
                nc.scalar.activation(S[0][par][:], y_ps[:], ACT.Silu, bias=consts[:, 1:2]).then_inc(S_ready[0], 1)

            def evacuate_l1(j, par):
                act.wait_ge(phi_used, l1_over(j))
                nc.scalar.activation(X[1][par][:], l1_ps[par][:], ACT.Relu, bias=xshift[:, 0:1],
                                     scale=XSCALE).then_inc(X_ready[1], 1)
                nc.scalar.activation(S[1][par][:], l1_ps[par][:], ACT.Silu).then_inc(S_ready[1], 1)

            def gelu(j, like):
                act.wait_ge(phi_used, l2_over(j))
                if like >= 1:
                    act.wait_ge(out_stored, 16 * j)
                nc.scalar.activation(act_out[:], l2_ps[:], ACT.Gelu).then_inc(gelu_ready, 1)

            def zigzag(half):
                m, layer, tile, par, rho = half
                f = fold[rho][:]
                if rho == 0:
                    act.wait_ge(X_ready[layer], tile + 1)
                    nc.scalar.activation(f, X[layer][par][:], ACT.Relu, bias=const[10][:], scale=-1.0)\
                        .then_inc(clip0_ready, 1)
                    act.wait_ge(clip0_ready, m + 1)
                else:
                    act.wait_ge(clip_ready, m + 1)
                for k, centre in enumerate((7 if rho else 4, 4, 2)):
                    nc.scalar.activation(f, f, ACT.Abs, bias=const[-centre][:]).then_inc(fold_ready, 1)
                    act.wait_ge(fold_ready, 6 * m + (3 * rho + k + 1))
                if not isinstance(m, int) or m >= 1:
                    act.wait_ge(F_ready, 4 * m + (2 * rho - 2))
                nc.scalar.activation(e_[rho][:], f, ACT.Identity, bias=const[-1][:]).then_inc(zigzag_ready, 1)
                nc.scalar.activation(q_[rho][:], f, ACT.Square, bias=const[-1][:]).then_inc(zigzag_ready, 1)
                nc.scalar.activation(g_[rho][:], f, ACT.Abs, bias=const[-2][:], scale=2.0).then_inc(zigzag_ready, 1)

            def step(i, like):
                now = halves(i, like)
                after = (now + (halves(i + 1, like + 1) if like < last else []))[1:]
                for k in range(len(now)):
                    if k < len(after):
                        zigzag(after[k])
                    if k == 1 and like >= 0 and like + 2 <= last:
                        evacuate_y(i + 2, like % 2, like)
                    if k == 1 and like >= 1:
                        gelu(i - 1, like - 1)
                    if k == min(2, len(now) - 1) and has_l1(like):
                        evacuate_l1(i + 1, (like + 1) % 2)

            act.wait_ge(shifts_ready, 6)
            evacuate_y(0, 0, -1)
            evacuate_y(1, 1, -1)
            zigzag(halves(first, first)[0])
            steps(act, step)
            gelu(last, last)

        @block.tensor
        def _(pe):
            def y(j, par, like):
                pe.wait_ge(x_loaded, 16 * (j + 1))
                pe.wait_ge(rows_loaded, 32 * (j + 1))
                pe.wait_ge(conv_ready, j + 1)
                if not isinstance(j, int) or j > 0:
                    pe.wait_ge(S_ready[0], j)
                src = tile_of(x_ring, j)
                for n in range(TN // MM):
                    nc.tensor.matmul(y_ps[:, n * MM:(n + 1) * MM], conv_t[:], src[:, n * MM:(n + 1) * MM],
                                     start=True, stop=False, skip_group_check=True)
                    for h in range(n * MM // W, (n + 1) * MM // W):
                        ins = nc.tensor.matmul(y_ps[:, h * W:(h + 1) * W], rows[:, par, h, :], inv_w_sb[:],
                                               start=False, stop=((h + 1) % (MM // W) == 0), skip_group_check=True)
                ins.then_inc(y_done, 1)

            def product(dst, layer, f, src):
                for n in range(TN // MM):
                    ins = nc.tensor.matmul(dst[:, n * MM:(n + 1) * MM], kan_w[layer][:, f, :],
                                           src[:, n * MM:(n + 1) * MM], start=(f == 0), stop=(f == NF - 1))
                return ins

            def step(i, like):
                if like >= 0 and like + 2 <= last:
                    y(i + 2, like % 2, like)
                for turn, layer, tile, par, rho in halves(i, like):
                    n = 2 * turn + rho
                    dst = l1_ps[par] if layer == 0 else l2_ps
                    if rho == 0:
                        pe.wait_ge(S_ready[layer], tile + 1)
                        if layer == 1 and like >= 1:
                            pe.wait_ge(gelu_ready, i)
                        product(dst, layer, 0, S[layer][par])
                    for m in range(4):
                        pe.wait_ge(phi_ready, 4 * n + m + 1)
                        ins = product(dst, layer, 1 + 4 * rho + m, phi[rho][m])
                    ins.then_inc(phi_used, 1)

            y(0, 0, -2)
            y(1, 1, -2)
            steps(pe, step)


_INS = ["x", "spec_w1_r", "spec_w1_i", "spec_w2_r", "spec_w2_i", "conv_w", "conv_b", "k1_base", "k1_spline",
        "k1_scaler", "k2_base", "k2_spline", "k2_scaler"]


def kernel(**inputs):
    import numpy as _np
    import concourse.bacc as _bacc
    from concourse import mybir as _mybir
    from concourse.bass_utils import run_bass_kernel_spmd as _run

    nc = _bacc.Bacc("TRN2", target_bir_lowering=False, num_devices=1)
    arrays, args = {}, []
    for name in _INS:
        a = _np.ascontiguousarray(inputs[name if name == "x" else f"L0_conv_{name}"])
        arrays[f"in_{name}_dram"] = a
        args.append(nc.dram_tensor(f"in_{name}_dram", a.shape, _mybir.dt.from_np(a.dtype), kind="ExternalInput").ap())
    for name, a in tables().items():
        arrays[f"{name}_dram"] = a
        args.append(nc.dram_tensor(f"{name}_dram", a.shape, _mybir.dt.from_np(a.dtype), kind="ExternalInput").ap())
    out = nc.dram_tensor("out_0_dram", (B, C, H, W), _mybir.dt.float32, kind="ExternalOutput").ap()
    build(nc, *args, out)
    r = _run(nc, [arrays], core_ids=[0])
    return r.results[0]["out_0_dram"]
```

```python
from contextlib import ExitStack

import numpy as np

import concourse.bass as bass
from concourse import mybir

F32 = mybir.dt.float32
ALU = mybir.AluOpType
ACT = mybir.ActivationFunctionType
AX = mybir.AxisListType

P = 128
B, C, H, W = 16, 64, 128, 128
G = 32
CG = C // G
MODES = 16
EPS = 1e-5
ORDER, GRID = 3, 5
KNOT = 2.0 / GRID
XSCALE = 1.0 / KNOT
XSHIFT = (1.0 + ORDER * KNOT) / KNOT
NB = GRID + ORDER
NF = 1 + NB

NS = MODES + 1
NU = 2 * MODES + 1
CH_GRP = 8
N_GRP = C // CH_GRP
MIX_ROWS = 8
MIX_BUFS = 3
MIX_CHUNKS = 2 * MODES // MIX_ROWS
S_BANK = 8

PAIRS = B // 2
TN = 1024
TH = TN // W
TILES_PAIR = H * W // TN
TILES = PAIRS * TILES_PAIR
MM = 512
RING = 4


def tables():
    h = np.arange(H, dtype=np.float64)
    w = np.arange(W, dtype=np.float64)
    k = np.arange(NS, dtype=np.float64)
    ky = np.arange(MODES, dtype=np.float64)
    ah = 2 * np.pi * np.outer(h, k) / H
    dft_h = np.concatenate([np.cos(ah), np.sin(ah)[:, 1:]], 1)
    aw = 2 * np.pi * np.outer(w, ky) / W
    c, s = np.cos(aw), np.sin(aw)
    dft_w = np.stack([np.concatenate([c, -s, c, -s], 1), np.concatenate([-s, -c, s, c], 1)], 1)
    kx = np.concatenate([np.arange(MODES), np.arange(-MODES, 0)]).astype(np.float64)
    ai = 2 * np.pi * np.outer(kx, h) / H
    inv_h = np.stack([np.stack([np.cos(ai), np.sin(ai)], 1), np.stack([-np.sin(ai), np.cos(ai)], 1)], 1)
    inv_h = inv_h.reshape(4 * MODES, 2, H)
    weight = np.where(ky == 0, 1.0, 2.0)[:, None] / (H * W)
    inv_w = np.concatenate([weight * c.T, -weight * s.T], 0)
    inv_w = np.concatenate([inv_w, inv_w], 0)
    pick = (np.arange(P)[:, None] % C // CG == np.arange(G)[None, :])
    return {n: np.ascontiguousarray(a, dtype=np.float32) for n, a in (
        ("dft_h", dft_h), ("dft_w", dft_w), ("inv_h", inv_h), ("inv_w", inv_w),
        ("pick", pick), ("ident", np.eye(C)))}


def build(nc, x, w1_r, w1_i, w2_r, w2_i, conv_w, conv_b, k1_base, k1_spline, k1_scaler,
          k2_base, k2_spline, k2_scaler, dft_h, dft_w, inv_h, inv_w, pick, ident, out):
    modes_dram = nc.dram_tensor("modes_scratch", [2 * MODES, 2 * B, MODES * C], F32, kind="Internal").ap()
    rows_dram = nc.dram_tensor("rows_scratch", [B, H, 2 * MODES * C], F32, kind="Internal").ap()

    with ExitStack() as keep:
        def held(name, shape):
            return keep.enter_context(nc.sbuf_tensor(name, shape, F32))

        kan_w = [held(f"kan_w{l}", [P, NF, P]) for l in range(2)]
        conv_blk = held("conv_blk", [P, P])
        conv_bias = held("conv_bias", [P, 1])
        inv_w_sb = held("inv_w_sb", [P // 2, W])
        pair_rs = held("pair_rs", [P, PAIRS])
        pair_consts = held("pair_consts", [P, PAIRS, 3])
        first_half(nc, locals())
        x_ring = held("x_ring", [P, RING, TN])
        rows_t = held("rows_t", [P // 2, 2, TH, P])
        x_loaded = keep.enter_context(nc.semaphore("x_loaded"))
        rows_loaded = keep.enter_context(nc.semaphore("rows_loaded"))
        inverse_rows(nc, locals())
        second_half(nc, locals())


def first_half(nc, t):
    with ExitStack() as ctx:
        def sb(name, shape):
            return ctx.enter_context(nc.sbuf_tensor(name, shape, F32))

        modes = sb("modes", [P, NS, 2, 2 * MODES, B])
        stats = sb("stats", [P, B, G, 6])
        t = dict(t, modes=modes, stats=stats)
        prepare_weights(nc, t)
        forward(nc, t)
        with ExitStack() as inner:
            t["rs_signed"] = inner.enter_context(nc.sbuf_tensor("rs_signed", [P, 2, B], F32))
            t["mix_w"] = [inner.enter_context(nc.sbuf_tensor(f"mix_w{i}", [P, C, MIX_ROWS, MODES], F32))
                          for i in range(MIX_BUFS)]
            t["modes_doubled"] = [inner.enter_context(nc.semaphore(f"modes_doubled{i}")) for i in range(2)]
            t["mix_loaded"] = [inner.enter_context(nc.semaphore(f"mix_loaded{k}")) for k in range(MIX_CHUNKS)]
            statistics(nc, t)
            mix_modes(nc, t)


def load_mix_part(nc, t, k, part, o0, n_o):
    half, rows = k // (MODES // MIX_ROWS), k % (MODES // MIX_ROWS) * MIX_ROWS
    src = ((t["w1_r"], t["w1_i"]), (t["w2_r"], t["w2_i"]))[half][part]
    nc.sync.dma_start(t["mix_w"][k % MIX_BUFS][part * C:(part + 1) * C, bass.ds(o0, n_o)],
                      src[:, bass.ds(o0, n_o), rows:rows + MIX_ROWS, :]).then_inc(t["mix_loaded"][k], 16)


def place(j):
    if isinstance(j, int):
        return j // TILES_PAIR, j % TILES_PAIR, j % RING, j % 2
    return (j >> 4) & (PAIRS - 1), j & (TILES_PAIR - 1), j & (RING - 1), j & 1


def tile_in_dram(a, pair, k):
    v = a.rearrange("(p i) c (t h) w -> p (i c) t (h w)", i=2, h=TH)
    return v[bass.ds(pair, 1), :, bass.ds(k, 1), :].rearrange("p c t n -> (p c) (t n)")


def load_tile(sp, t, where):
    pair, k, slot, par = where
    sp.dma_start(t["x_ring"][:, bass.ds(slot, 1), :].rearrange("p a n -> p (a n)"),
                 tile_in_dram(t["x"], pair, k)).then_inc(t["x_loaded"], 16)
    for i in range(2):
        src = t["rows_dram"].rearrange("(p i) (t h) (q o) -> p i t q h o", i=2, h=TH, o=C)
        src = src[bass.ds(pair, 1), i, bass.ds(k, 1), :, :, :].rearrange("p t q h o -> (p t q) h o")
        dst = t["rows_t"][i * 2 * MODES:(i + 1) * 2 * MODES, bass.ds(par, 1), :, i * C:(i + 1) * C]
        sp.dma_start(dst.rearrange("q a h o -> q (a h) o"), src).then_inc(t["rows_loaded"], 16)


def prepare_weights(nc, t):
    conv_blk, conv_bias, kan_w, inv_w_sb = t["conv_blk"], t["conv_bias"], t["kan_w"], t["inv_w_sb"]
    with ExitStack() as ctx:
        def sb(name, shape):
            return ctx.enter_context(nc.sbuf_tensor(name, shape, F32))

        def sem(name):
            return ctx.enter_context(nc.semaphore(name))

        spline = [sb(f"spline{l}", [C, C, NB]) for l in range(2)]
        scaler = [sb(f"scaler{l}", [C, C]) for l in range(2)]
        mats = [sb(f"mats{l}", [C, NF, 2, C]) for l in range(2)]
        conv_nat = sb("conv_nat", [C, 2, C])
        eye = sb("eye", [C, C])
        turned = [ctx.enter_context(nc.psum_tensor(f"turned{i}", [P, C], F32)) for i in range(2)]
        natural_loaded, consts_loaded = sem("natural_loaded"), sem("consts_loaded")
        scaled, sixth, mixed, cleared = sem("scaled"), sem("sixth"), sem("mixed"), sem("cleared")
        turn_done, turn_kept = sem("turn_done"), sem("turn_kept")
        n_natural = 0
        jobs = [(l, f) for l in range(2) for f in range(NF)] + [(None, 0)]

        block = ctx.enter_context(nc.Block())

        @block.sync
        def _(sp):
            loads = [(eye[:], t["ident"])]
            for l, (b_, s_, c_) in enumerate(((t["k1_base"], t["k1_spline"], t["k1_scaler"]),
                                              (t["k2_base"], t["k2_spline"], t["k2_scaler"]))):
                loads += [(spline[l][:], s_), (scaler[l][:], c_)]
                loads += [(mats[l][:, 0, d, :], b_) for d in range(2)]
            loads += [(conv_nat[:, d, :], t["conv_w"]) for d in range(2)]
            for dst, src in loads:
                sp.dma_start(dst, src).then_inc(natural_loaded, 16)
            for d in range(2):
                sp.dma_start(conv_bias[d * C:(d + 1) * C, :],
                             t["conv_b"].rearrange("(c a) -> c a", a=1)).then_inc(consts_loaded, 16)
            sp.dma_start(inv_w_sb[:], t["inv_w"]).then_inc(consts_loaded, 16)
            sp.wait_ge(natural_loaded, 16 * len(loads))
            sp.wait_ge(consts_loaded, 48)

        n_loads = 1 + 2 * 4 + 2

        @block.vector
        def _(dve):
            nc.vector.memset(kan_w[0][:], 0.0).then_inc(cleared, 1)
            nc.vector.memset(kan_w[1][:], 0.0).then_inc(cleared, 1)
            nc.vector.memset(conv_blk[:], 0.0).then_inc(cleared, 1)
            dve.wait_ge(natural_loaded, 16 * n_loads)
            for l in range(2):
                nc.vector.scalar_tensor_tensor(
                    out=spline[l][:], in0=spline[l][:], scalar=1.0 / 6.0,
                    in1=scaler[l][:].unsqueeze(2).to_broadcast([C, C, NB]),
                    op0=ALU.mult, op1=ALU.mult).then_inc(scaled, 1)
            for l in range(2):
                dve.wait_ge(scaled, l + 1)
                w = [spline[l][:, :, k] for k in range(NB)]
                for rho in range(2):
                    f = 1 + 4 * rho
                    for d in range(2):
                        m = mats[l][:, :, d, :]
                        nc.vector.tensor_tensor(m[:, f, :], w[rho + 4], w[rho], ALU.subtract).then_inc(mixed, 1)
                        nc.vector.tensor_scalar(m[:, f + 1, :], w[rho + 4], -1.0, None, ALU.mult).then_inc(mixed, 1)
                        nc.vector.tensor_copy(m[:, f + 2, :], w[rho + 2]).then_inc(mixed, 1)
                        nc.vector.tensor_tensor(m[:, f + 3, :], w[rho + 6], w[rho + 2], ALU.subtract).then_inc(mixed, 1)
            dve.wait_ge(cleared, 3)
            for n, (l, f) in enumerate(jobs):
                dst = conv_blk[:] if l is None else kan_w[l][:, f, :]
                dve.wait_ge(turn_done, n + 1)
                nc.vector.tensor_copy(dst[0:C, 0:C], turned[n % 2][0:C, :])
                nc.vector.tensor_copy(dst[C:P, C:P], turned[n % 2][C:P, :]).then_inc(turn_kept, 1)

        @block.tensor
        def _(pe):
            pe.wait_ge(natural_loaded, 16 * n_loads)
            pe.wait_ge(mixed, 2 * 2 * 2 * 4)
            for n, (l, f) in enumerate(jobs):
                src = conv_nat[:] if l is None else mats[l][:, f, :, :]
                if n >= 2:
                    pe.wait_ge(turn_kept, n - 1)
                nc.tensor.matmul(turned[n % 2][:], src.rearrange("o d i -> o (d i)"), eye[:],
                                 start=True, stop=True).then_inc(turn_done, 1)


def forward(nc, t):
    modes, stats = t["modes"], t["stats"]
    with ExitStack() as ctx:
        def sb(name, shape):
            return ctx.enter_context(nc.sbuf_tensor(name, shape, F32))

        def sem(name):
            return ctx.enter_context(nc.semaphore(name))

        PARTS = 8
        QC = C // PARTS
        img = sb("img", [P, 2, C, W])
        freq = sb("freq", [P, 2, NU, C])
        dft_h_sb = sb("dft_h_sb", [P, NU])
        dft_w_sb = sb("dft_w_sb", [P, 2, 4 * MODES])
        along_h = [ctx.enter_context(nc.psum_tensor(f"along_h{i}", [P, CH_GRP, NU], F32)) for i in range(4)]
        along_w = [ctx.enter_context(nc.psum_tensor(f"along_w{i}", [C, S_BANK, 2, 2 * MODES], F32)) for i in range(3)]
        img_loaded = [[sem(f"img_loaded{p}{q}") for q in range(PARTS)] for p in range(2)]
        tables_loaded = sem("tables_loaded")
        along_h_done = sem("along_h_done")
        freq_ready = sem("freq_ready")
        along_w_done = sem("along_w_done")
        modes_kept = sem("modes_kept")

        block = ctx.enter_context(nc.Block())

        @block.sync
        def _(sp):
            def load(par, b):
                for q in range(PARTS):
                    src = t["x"][b].rearrange("c h w -> h c w") if isinstance(b, int) else \
                        t["x"][bass.ds(b, 1)].rearrange("a c h w -> h (a c) w")
                    sp.dma_start(img[:, par, q * QC:(q + 1) * QC, :],
                                 src[:, q * QC:(q + 1) * QC, :]).then_inc(img_loaded[par][q], 16)

            sp.dma_start(dft_h_sb[:], t["dft_h"]).then_inc(tables_loaded, 16)
            sp.dma_start(dft_w_sb[:], t["dft_w"]).then_inc(tables_loaded, 16)
            load(0, 0)
            load(1, 1)
            with sp.Fori(1, B // 2) as b2:
                for par in range(2):
                    sp.wait_ge(modes_kept, 2 * b2 + par)
                    load(par, 2 * b2 + par)

        @block.vector
        def _(dve):
            with dve.Fori(0, B // 2) as b2:
                for par in range(2):
                    b = 2 * b2 + par
                    for q in range(PARTS):
                        dve.wait_ge(img_loaded[par][q], 16 * (b2 + 1))
                        for g in range(q * QC // CG, (q + 1) * QC // CG):
                            ins = nc.vector.bn_stats(stats[:, bass.ds(b, 1), g, :],
                                                     img[:, par, CG * g:CG * (g + 1), :].rearrange("p c w -> p (c w)"))
                    dve.wait_ge(along_w_done, b + 1)
                    for i in range(3):
                        n = min(S_BANK, NS - S_BANK * i)
                        ins = nc.vector.tensor_copy(
                            modes[0:C, S_BANK * i:S_BANK * i + n, :, :, bass.ds(b, 1)].rearrange("p s g m b -> p (s g m) b"),
                            along_w[i][:, 0:n, :, :].rearrange("p s g (m b) -> p (s g m) b", b=1))
                    ins.then_inc(modes_kept, 1)

        @block.tensor
        def _(pe):
            pe.sem_inc(modes_kept, 1)
            pe.wait_ge(tables_loaded, 32)
            with pe.Fori(0, B // 2) as b2:
                for par in range(2):
                    b = 2 * b2 + par
                    for g in range(N_GRP):
                        if g % (QC // CH_GRP) == 0:
                            pe.wait_ge(img_loaded[par][g * CH_GRP // QC], 16 * (b2 + 1))
                        pe.wait_ge(freq_ready, N_GRP * b + (g + 1))
                        for c in range(CH_GRP):
                            ins = nc.tensor.matmul(along_h[g % 4][:, c, :], img[:, par, CH_GRP * g + c, :],
                                                   dft_h_sb[:], start=True, stop=True)
                        ins.then_inc(along_h_done, 1)
                    pe.wait_ge(freq_ready, N_GRP * b + (N_GRP + 4))
                    pe.wait_ge(modes_kept, b + 1)
                    for s in range(NS):
                        dst = along_w[s // S_BANK][:, s % S_BANK, :, :].rearrange("p g m -> p (g m)")
                        ins = nc.tensor.matmul(dst, freq[:, par, s, :], dft_w_sb[:, 0, :],
                                               start=True, stop=(s == 0))
                        if s > 0:
                            ins = nc.tensor.matmul(dst, freq[:, par, MODES + s, :], dft_w_sb[:, 1, :],
                                                   start=False, stop=True)
                    ins.then_inc(along_w_done, 1)

        @block.scalar
        def _(act):
            act.sem_inc(freq_ready, 4)
            with act.Fori(0, B // 2) as b2:
                for par in range(2):
                    b = 2 * b2 + par
                    for g in range(N_GRP):
                        act.wait_ge(along_h_done, N_GRP * b + (g + 1))
                        nc.scalar.activation(freq[:, par, :, CH_GRP * g:CH_GRP * (g + 1)],
                                             along_h[g % 4][:].rearrange("p c u -> p u c"),
                                             ACT.Copy).then_inc(freq_ready, 1)


def statistics(nc, t):
    modes, stats = t["modes"], t["stats"]
    conv_blk, conv_bias, pair_rs, pair_consts = t["conv_blk"], t["conv_bias"], t["pair_rs"], t["pair_consts"]
    with ExitStack() as ctx:
        def sb(name, shape):
            return ctx.enter_context(nc.sbuf_tensor(name, shape, F32))

        def sem(name):
            return ctx.enter_context(nc.semaphore(name))

        mean_all = sb("mean_all", [P, 1])
        avg = sb("avg", [P, P])
        avg_sq = sb("avg_sq", [P, P])
        pick_sb = sb("pick_sb", [P, G])
        mean_bg = sb("mean_bg", [P, B, G])
        dev = sb("dev", [P, 2, B, G])
        dev_sq = sb("dev_sq", [P, 2, B, G])
        picked = sb("picked", [P, 2, B, G])
        var = sb("var", [P, B])
        root = sb("root", [P, B])
        quot = sb("quot", [P, B])
        doubled = sb("doubled", [P, B])
        rs_c = sb("rs_c", [P, B])
        mean_c = sb("mean_c", [P, B])
        pair_rm = sb("pair_rm", [P, PAIRS])
        pair_mean = sb("pair_mean", [P, PAIRS])
        ps_mean = ctx.enter_context(nc.psum_tensor("ps_mean", [P, B, G], F32))
        ps_var = ctx.enter_context(nc.psum_tensor("ps_var", [P, B, G], F32))
        ps_bias = ctx.enter_context(nc.psum_tensor("ps_bias", [P, PAIRS], F32))
        pick_loaded, set_up = sem("pick_loaded"), sem("set_up")
        mean_done, dev_ready, var_done = sem("mean_done"), sem("dev_ready"), sem("var_done")
        var_ready, root_ready, chain = sem("var_ready"), sem("root_ready"), sem("chain")
        rm_ready, bias_done = sem("rm_ready"), sem("bias_done")
        block = ctx.enter_context(nc.Block())

        @block.sync
        def _(sp):
            sp.dma_start(pick_sb[:], t["pick"]).then_inc(pick_loaded, 16)
            for k, ss in enumerate((slice(0, S_BANK), slice(S_BANK, NS))):
                for part in range(2):
                    src = modes[0:C, ss, :, part * MODES:(part + 1) * MODES, :]
                    dst = modes[C:P, ss, :, (1 - part) * MODES:(2 - part) * MODES, :]
                    sp.dma_start(dst.rearrange("p s g k b -> p (s g) (k b)"),
                                 src.rearrange("p s g k b -> p (s g) (k b)")).then_inc(t["modes_doubled"][k], 16)
                for part in range(2):
                    load_mix_part(nc, t, k, part, 0, C)

        @block.tensor
        def _(pe):
            pe.wait_ge(set_up, 2)
            for eo in range(2):
                ins = nc.tensor.matmul(ps_mean[:], avg[:], stats[:, :, :, 3 * eo + 1], start=(eo == 0), stop=(eo == 1))
            ins.then_inc(mean_done, 1)
            pe.wait_ge(dev_ready, 1)
            for eo in range(2):
                nc.tensor.matmul(ps_var[:], avg_sq[:], stats[:, :, :, 3 * eo + 2], start=(eo == 0), stop=False)
            for eo in range(2):
                ins = nc.tensor.matmul(ps_var[:], avg_sq[:], dev_sq[:, eo], start=False, stop=(eo == 1))
            ins.then_inc(var_done, 1)
            pe.wait_ge(rm_ready, 1)
            nc.tensor.matmul(ps_bias[:], conv_blk[:], pair_rm[:], start=True, stop=True).then_inc(bias_done, 1)

        @block.scalar
        def _(act):
            act.wait_ge(var_ready, 1)
            nc.scalar.activation(root[:], var[:], ACT.Sqrt).then_inc(root_ready, 1)

        @block.vector
        def _(dve):
            links = [0]

            def link(ins):
                links[0] += 1
                ins.then_inc(chain, 1)
                dve.wait_ge(chain, links[0])

            nc.vector.memset(avg[:], 0.5 / P).then_inc(set_up, 1)
            nc.vector.memset(avg_sq[:], 1.0 / (CG * H * W)).then_inc(set_up, 1)
            dve.wait_ge(mean_done, 1)
            link(nc.vector.tensor_copy(mean_bg[:], ps_mean[:]))
            for eo in range(2):
                link(nc.vector.tensor_tensor(dev[:, eo], stats[:, :, :, 3 * eo + 1], mean_bg[:], ALU.subtract))
            n_half = CG * W // 2
            nc.vector.scalar_tensor_tensor(out=dev_sq[:], in0=dev[:], scalar=float(n_half), in1=dev[:],
                                           op0=ALU.mult, op1=ALU.mult).then_inc(dev_ready, 1)

            def pick_own(k, src, dst):
                link(nc.vector.tensor_tensor(picked[:, k], src[:], pick_sb[:].unsqueeze(1).to_broadcast([P, B, G]),
                                             ALU.mult))
                link(nc.vector.tensor_reduce(dst[:], picked[:, k], AX.X, ALU.add))

            dve.wait_ge(pick_loaded, 16)
            pick_own(0, mean_bg, mean_c)
            dve.wait_ge(var_done, 1)
            pick_own(1, ps_var, var)
            link(nc.vector.tensor_scalar(var[:], var[:], EPS, None, ALU.add))
            dve.sem_inc(var_ready, 1)
            dve.wait_ge(root_ready, 1)
            link(nc.vector.reciprocal(quot[:], root[:]))
            link(nc.vector.tensor_tensor(quot[:], quot[:], var[:], ALU.mult))
            link(nc.vector.tensor_tensor(doubled[:], quot[:], root[:], ALU.add))
            link(nc.vector.tensor_scalar(doubled[:], doubled[:], 0.5, None, ALU.mult))
            link(nc.vector.reciprocal(rs_c[:], doubled[:]))
            for half in range(2):
                rows = slice(half * C, (half + 1) * C)
                link(nc.vector.tensor_copy(pair_rs[rows, :], rs_c[rows, half:B:2]))
                link(nc.vector.tensor_copy(pair_mean[rows, :], mean_c[rows, half:B:2]))
            nc.vector.tensor_tensor(pair_rm[:], pair_rs[:], pair_mean[:], ALU.mult).then_inc(rm_ready, 1)
            dve.wait_ge(bias_done, 1)
            link(nc.vector.tensor_copy(pair_consts[:, :, 0], pair_rs[:]))
            link(nc.vector.tensor_scalar(pair_consts[:, :, 1], ps_bias[:], -1.0, conv_bias[:, 0:1], ALU.mult, ALU.add))
            link(nc.vector.tensor_scalar(pair_consts[:, :, 2], pair_consts[:, :, 1], XSCALE, XSHIFT, ALU.mult, ALU.add))
            for part in range(2):
                link(nc.vector.tensor_copy(t["rs_signed"][:, part, :], rs_c[:]))
            link(nc.vector.tensor_scalar(t["rs_signed"][C:P, 0, :], rs_c[C:P, :], -1.0, None, ALU.mult))
            dve.wait_ge(t["modes_doubled"][0], 32)
            for half in range(2):
                rows = slice(half * C, (half + 1) * C)
                dc = modes[rows, 0, 0, half * MODES, :]
                link(nc.vector.scalar_tensor_tensor(out=dc, in0=mean_c[rows, :], scalar=-float(H * W), in1=dc,
                                                    op0=ALU.mult, op1=ALU.add))


def mix_modes(nc, t):
    modes, modes_dram, rs_signed = t["modes"], t["modes_dram"], t["rs_signed"]
    with ExitStack() as ctx:
        def sb(name, shape):
            return ctx.enter_context(nc.sbuf_tensor(name, shape, F32))

        def sem(name):
            return ctx.enter_context(nc.semaphore(name))

        normed = [sb(f"normed{i}", [P, MODES + 1, 2, B]) for i in range(2)]
        mixed = [sb(f"mixed{i}", [2 * B, MODES * C]) for i in range(2)]
        ps = [ctx.enter_context(nc.psum_tensor(f"mix_ps{i}", [C, 2, MM], F32)) for i in range(2)]
        cleared = sem("mix_cleared")
        normed_ready, mix_done, mix_kept = sem("normed_ready"), sem("mix_done"), sem("mix_kept")
        stored = [sem(f"mix_stored{i}") for i in range(2)]
        block = ctx.enter_context(nc.Block())
        CHUNK = MIX_ROWS // 2

        @block.vector
        def _(dve):
            nc.vector.memset(normed[0][:, MODES, :, :], 0.0).then_inc(cleared, 1)
            nc.vector.memset(normed[1][:, MODES, :, :], 0.0).then_inc(cleared, 1)
            for quarter in range(4):
                half, x0 = quarter // 2, quarter % 2 * S_BANK
                if quarter == 1:
                    dve.wait_ge(t["modes_doubled"][1], 32)
                with dve.Fori(0, S_BANK // 2) as x2:
                    for u in range(2):
                        xx = 2 * x2 + (u + x0)
                        s = xx if half == 0 else xx * -1 + MODES
                        dve.wait_ge(mix_done, xx + (MODES * half + 1))
                        nc.vector.tensor_tensor(
                            normed[u][:, 0:MODES, :, :].rearrange("p k r b -> p r k b"),
                            modes[:, bass.ds(s, 1), half, :, :].rearrange("p s (r k) b -> p (s r) k b", r=2),
                            rs_signed[:].unsqueeze(2).to_broadcast([P, 2, MODES, B]),
                            ALU.mult).then_inc(normed_ready, 1)

        @block.tensor
        def _(pe):
            pe.sem_inc(mix_done, 2)
            pe.wait_ge(cleared, 2)
            for k in range(MIX_CHUNKS):
                pe.wait_ge(t["mix_loaded"][k], 32 if k < 2 else 16 * MIX_ROWS)
                with pe.Fori(0, CHUNK) as x2:
                    for u in range(2):
                        row = 2 * x2 + u
                        pe.wait_ge(normed_ready, row + (MIX_ROWS * k + 1))
                        pe.wait_ge(mix_kept, row + (MIX_ROWS * k + 1))
                        for ky in range(MODES):
                            ins = nc.tensor.matmul(
                                ps[u][:, ky // 8, (ky % 8) * C:(ky % 8 + 1) * C],
                                normed[u][:, ky:ky + 2, :, :].rearrange("p k r b -> p (k r b)"),
                                t["mix_w"][k % MIX_BUFS][:, :, bass.ds(row, 1), ky].rearrange("p o x -> p (o x)"),
                                start=True, stop=True)
                        ins.then_inc(mix_done, 1)

        @block.scalar
        def _(act):
            act.sem_inc(mix_kept, 2)
            act.sem_inc(stored[0], 16)
            act.sem_inc(stored[1], 16)
            with act.Fori(0, MODES) as x2:
                for u in range(2):
                    act.wait_ge(mix_done, 2 * x2 + (u + 3))
                    act.wait_ge(stored[u], 16 * (x2 + 1))
                    nc.scalar.activation(mixed[u][:], ps[u][0:2 * B, :, :].rearrange("p a n -> p (a n)"),
                                         ACT.Copy).then_inc(mix_kept, 1)

        @block.sync
        def _(sp):
            for k in range(MIX_CHUNKS):
                if MIX_BUFS <= k + 2 < MIX_CHUNKS:
                    sp.wait_ge(mix_done, MIX_ROWS * k + 2)
                with sp.Fori(0, CHUNK) as x2:
                    for u in range(2):
                        n = 2 * x2 + (u + MIX_ROWS * k)
                        sp.wait_ge(mix_kept, n + 3)
                        sp.dma_start(modes_dram[bass.ds(n, 1)].rearrange("a q f -> (a q) f"),
                                     mixed[u][:]).then_inc(stored[u], 16)
                        if k + 2 < MIX_CHUNKS:
                            load_mix_part(nc, t, k + 2, u, x2 * (C // CHUNK), C // CHUNK)
            for u in range(2):
                sp.wait_ge(stored[u], 16 * (MODES + 1))


def inverse_rows(nc, t):
    modes_dram, rows_dram = t["modes_dram"], t["rows_dram"]
    with ExitStack() as ctx:
        def sb(name, shape):
            return ctx.enter_context(nc.sbuf_tensor(name, shape, F32))

        def sem(name):
            return ctx.enter_context(nc.semaphore(name))

        K = 4 * MODES
        BANKS = 2 * MODES * C // MM
        inv_h_sb = [sb(f"inv_h_sb{u}", [2 * K, 2, H]) for u in range(2)]
        spec = [sb(f"spec{p}", [2 * K, MODES * C]) for p in range(2)]
        rows = [[sb(f"rows{p}{u}", [H, 2 * MODES * C]) for u in range(2)] for p in range(2)]
        ps = [[ctx.enter_context(nc.psum_tensor(f"rows_ps{u}{k}", [H, MM], F32)) for k in range(BANKS)]
              for u in range(2)]
        inv_h_loaded, inv_h_zero, tiles_zero = sem("inv_h_loaded"), sem("inv_h_zero"), sem("tiles_zero")
        spec_loaded = [sem(f"spec_loaded{p}") for p in range(2)]
        rows_done = [sem(f"rows_done{u}") for u in range(2)]
        rows_kept = [sem(f"rows_kept{u}") for u in range(2)]
        rows_stored = [[sem(f"rows_stored{p}{u}") for u in range(2)] for p in range(2)]
        src = modes_dram.rearrange("k (q b) f -> (k q) b f", b=B)
        block = ctx.enter_context(nc.Block())

        @block.sync
        def _(sp):
            def load(pair, p):
                for u in range(2):
                    sp.dma_start(spec[p][u * K:(u + 1) * K, :],
                                 src[:, bass.ds(2 * pair + u, 1), :].rearrange("k b f -> k (b f)"))\
                      .then_inc(spec_loaded[p], 16)

            def store(pair, p, u):
                sp.dma_start(rows_dram[bass.ds(2 * pair + u, 1)].rearrange("a h f -> (a h) f"),
                             rows[p][u][:]).then_inc(rows_stored[p][u], 16)

            for u in range(2):
                sp.dma_start(inv_h_sb[u][u * K:(u + 1) * K], t["inv_h"]).then_inc(inv_h_loaded, 16)
            load(0, 0)
            load(1, 1)
            with sp.Fori(0, PAIRS // 2 - 1) as pair2:
                for p in range(2):
                    pair = 2 * pair2 + p
                    for u in range(2):
                        sp.wait_ge(rows_kept[u], BANKS * pair + 2 * BANKS)
                        store(pair, p, u)
                    load(pair + 2, p)
            sp.wait_ge(tiles_zero, 1)
            for u in range(2):
                sp.wait_ge(rows_stored[0][u], 32)
            load_tile(sp, t, place(0))
            for pair in range(PAIRS - 2, PAIRS):
                for u in range(2):
                    sp.wait_ge(rows_kept[u], BANKS * (pair + 2))
                    store(pair, pair % 2, u)
                if pair == PAIRS - 2:
                    sp.wait_ge(t["x_loaded"], 16)
                    sp.wait_ge(t["rows_loaded"], 32)
                    load_tile(sp, t, place(1))
            for p in range(2):
                for u in range(2):
                    sp.wait_ge(rows_stored[p][u], 16 * (PAIRS // 2 + 1))

        @block.tensor
        def _(pe):
            pe.wait_ge(inv_h_loaded, 32)
            pe.wait_ge(inv_h_zero, 2)
            with pe.Fori(0, PAIRS // 2) as pair2:
                for p in range(2):
                    pair = 2 * pair2 + p
                    pe.wait_ge(spec_loaded[p], 32 * (pair2 + 1))
                    for k in range(BANKS):
                        for u in range(2):
                            pe.wait_ge(rows_kept[u], BANKS * pair + (k + 1))
                            part, cols = k // (BANKS // 2), k % (BANKS // 2) * MM
                            nc.tensor.matmul(ps[u][k][:], inv_h_sb[u][:, part, :], spec[p][:, cols:cols + MM],
                                             start=True, stop=True).then_inc(rows_done[u], 1)

        def keep(eng, u, copy):
            eng.sem_inc(rows_kept[u], BANKS)
            for p in range(2):
                eng.sem_inc(rows_stored[p][u], 16)
            with eng.Fori(0, PAIRS // 2) as pair2:
                for p in range(2):
                    eng.wait_ge(rows_stored[p][u], 16 * (pair2 + 1))
                    for k in range(BANKS):
                        eng.wait_ge(rows_done[u], 2 * BANKS * pair2 + (BANKS * p + k + 1))
                        copy(rows[p][u][:, k * MM:(k + 1) * MM], ps[u][k][:]).then_inc(rows_kept[u], 1)

        @block.scalar
        def _(act):
            keep(act, 0, lambda dst, src_: nc.scalar.activation(dst, src_, ACT.Copy))

        @block.vector
        def _(dve):
            for u in range(2):
                other = slice((1 - u) * K, (2 - u) * K)
                nc.vector.memset(inv_h_sb[u][other], 0.0).then_inc(inv_h_zero, 1)
            nc.vector.memset(t["rows_t"][:], 0.0).then_inc(tiles_zero, 1)
            keep(dve, 1, nc.vector.tensor_copy)


def second_half(nc, t):
    out, kan_w, conv_blk, inv_w_sb, pair_consts = (
        t[n] for n in ("out", "kan_w", "conv_blk", "inv_w_sb", "pair_consts"))
    x_ring, rows, x_loaded, rows_loaded = (t[n] for n in ("x_ring", "rows_t", "x_loaded", "rows_loaded"))
    with ExitStack() as ctx:
        def sb(name, shape):
            return ctx.enter_context(nc.sbuf_tensor(name, shape, F32))

        def ps(name):
            return ctx.enter_context(nc.psum_tensor(name, [P, TN], F32))

        def sem(name):
            return ctx.enter_context(nc.semaphore(name))

        consts = sb("consts", [P, 3])
        conv_t = sb("conv_t", [P, P])
        X = [[sb(f"X{l}{p}", [P, TN]) for p in range(2)] for l in range(2)]
        S = [[sb(f"S{l}{p}", [P, TN]) for p in range(2)] for l in range(2)]
        fold = [sb(f"fold{p}", [P, TN]) for p in range(2)]
        e_ = [sb(f"e{p}", [P, TN]) for p in range(2)]
        g_ = [sb(f"g{p}", [P, TN]) for p in range(2)]
        q_ = [sb(f"q{p}", [P, TN]) for p in range(2)]
        F1, F2, Cn, Cp = ([sb(f"{name}{p}", [P, TN]) for p in range(2)] for name in ("F1_", "F2_", "Cn", "Cp"))
        phi = [[sb(f"phi{p}{m}", [P, TN]) for m in range(4)] for p in range(2)]
        act_out = sb("act_out", [P, TN])
        const = {v: sb(f"const{v}".replace("-", "m"), [P, 1]) for v in (-1, -2, -4, -7, 10)}
        xshift = sb("xshift", [P, 1])
        y_ps, l2_ps = ps("y_ps"), ps("l2_ps")
        l1_ps = [ps("l1_ps0"), ps("l1_ps1")]

        out_stored = sem("out_stored")
        consts_ready, conv_ready = sem("consts_ready"), sem("conv_ready")
        y_done = sem("y_done")
        X_ready = [sem("X0_ready"), sem("X1_ready")]
        S_ready = [sem("S0_ready"), sem("S1_ready")]
        shifts_ready = sem("shifts_ready")
        gelu_ready = sem("gelu_ready")
        x_added = sem("x_added")
        clip_ready = sem("clip_ready")
        clip0_ready = sem("clip0_ready")
        fold_ready = sem("fold_ready")
        zigzag_ready = sem("zigzag_ready")
        F_ready, C_ready = sem("F_ready"), sem("C_ready")
        phi_ready = sem("phi_ready")
        phi_used = sem("phi_used")

        first, last = -1, TILES - 1
        LOOP0, LOOP1 = 2, TILES - 4
        assert (LOOP1 - LOOP0) % 2 == 0

        def steps(eng, body):
            for i in range(first, LOOP0):
                body(i, i)
            with eng.Fori(0, (LOOP1 - LOOP0) // 2) as turn:
                for u in range(2):
                    body(2 * turn + (LOOP0 + u), LOOP0 + u)
            for i in range(LOOP1, last + 1):
                body(i, i)

        def l1_over(j):
            return 2 if isinstance(j, int) and j == 0 else 4 * j

        def l2_over(j):
            return 4 * TILES if isinstance(j, int) and j == last else 4 * j + 6

        def has_l1(like):
            return like + 1 <= last

        def has_l2(like):
            return like >= 0

        def halves(i, like):
            found = []
            m = 2 * i + 1 if like >= 0 else 0
            if has_l1(like):
                found += [(m, 0, i + 1, (like + 1) % 2, rho) for rho in range(2)]
                m = m + 1
            if has_l2(like):
                found += [(m, 1, i, like % 2, rho) for rho in range(2)]
            return found

        def tile_of(ring, j):
            slot = j % RING if isinstance(j, int) else j & (RING - 1)
            return ring[:, slot, :] if isinstance(slot, int) else ring[:, bass.ds(slot, 1), :].rearrange("p a n -> p (a n)")

        block = ctx.enter_context(nc.Block())

        @block.sync
        def _(sp):
            def store(where):
                sp.dma_start(tile_in_dram(out, *where[:2]), act_out[:]).then_inc(out_stored, 16)

            for j in range(2, RING):
                sp.wait_ge(y_done, j)
                load_tile(sp, t, place(j))
            with sp.Fori(1, TILES - RING + 1) as i:
                stored, loaded = place(i - 1), place(i + (RING - 1))
                sp.wait_ge(x_added, 16 * i)
                store(stored)
                load_tile(sp, t, loaded)
            for j in range(TILES - RING, TILES):
                sp.wait_ge(x_added, 16 * (j + 1))
                store(place(j))
            sp.wait_ge(out_stored, 16 * TILES)

        @block.gpsimd
        def _(pool):
            def prepare(j):
                if not isinstance(j, int) or j > 0:
                    pool.wait_ge(S_ready[0], j)
                pair = j // TILES_PAIR if isinstance(j, int) else (j >> 4) & (PAIRS - 1)
                nc.gpsimd.tensor_copy(consts[:], pair_consts[:, bass.ds(pair, 1), :].rearrange("p a k -> p (a k)"))\
                    .then_inc(consts_ready, 1)
                pool.wait_ge(consts_ready, j + 1)
                nc.gpsimd.tensor_tensor(conv_t[:], conv_blk[:], consts[:, 0:1].to_broadcast([P, P]),
                                        ALU.mult).then_inc(conv_ready, 1)

            def add_residual(j):
                pool.wait_ge(gelu_ready, j + 1)
                pool.dma_start(act_out[:], tile_of(x_ring, j), accum_op=ALU.add).then_inc(x_added, 16)

            for j in range(4):
                prepare(j)
            with pool.Fori(0, TILES - 4) as j:
                add_residual(j)
                prepare(j + 4)
            for j in range(TILES - 4, TILES):
                add_residual(j)

        @block.vector
        def _(dve):
            def clip(half):
                m, layer, tile, par, rho = half
                if rho == 0:
                    return
                dve.wait_ge(X_ready[layer], tile + 1)
                nc.vector.tensor_scalar(fold[rho][:], X[layer][par][:], float(rho), float(rho + 10),
                                        ALU.max, ALU.min).then_inc(clip_ready, 1)

            def polynomials(half):
                turn, layer, tile, par, rho = half
                dve.wait_ge(zigzag_ready, 6 * turn + (3 * rho + 3))
                nc.vector.scalar_tensor_tensor(out=F1[rho][:], in0=q_[rho][:], scalar=3.0, in1=e_[rho][:],
                                               op0=ALU.subtract, op1=ALU.mult).then_inc(F_ready, 1)
                nc.vector.scalar_tensor_tensor(out=F2[rho][:], in0=g_[rho][:], scalar=3.0, in1=q_[rho][:],
                                               op0=ALU.subtract, op1=ALU.mult).then_inc(F_ready, 1)

            def bases(half):
                turn, layer, tile, par, rho = half
                dve.wait_ge(F_ready, 4 * turn + (2 * rho + 2))
                nc.vector.scalar_tensor_tensor(out=Cn[rho][:], in0=F1[rho][:], scalar=1.0, in1=F2[rho][:],
                                               op0=ALU.subtract, op1=ALU.add).then_inc(C_ready, 1)
                nc.vector.scalar_tensor_tensor(out=Cp[rho][:], in0=F1[rho][:], scalar=1.0, in1=F2[rho][:],
                                               op0=ALU.add, op1=ALU.subtract).then_inc(C_ready, 1)

            def cut(half, like, m):
                turn, layer, tile, par, rho = half
                if like >= 0 and m == 0:
                    dve.wait_ge(phi_used, 2 * turn + (rho - 1))
                dve.wait_ge(C_ready, 4 * turn + (2 * rho + 1 + m // 2))
                knot, op, src = ((4, ALU.is_lt, Cn), (8, ALU.is_lt, Cn), (2, ALU.is_ge, Cp), (6, ALU.is_ge, Cp))[m]
                nc.vector.scalar_tensor_tensor(out=phi[rho][m][:], in0=X[layer][par][:], scalar=float(rho + knot),
                                               in1=src[rho][:], op0=op, op1=ALU.mult).then_inc(phi_ready, 1)

            def step(i, like):
                later = halves(i, like) + (halves(i + 1, like + 1) if like < last else [])
                for k, half in enumerate(halves(i, like)):
                    if k + 2 < len(later):
                        clip(later[k + 2])
                    bases(half)
                    for m in range(3):
                        cut(half, like, m)
                    if k + 1 < len(later):
                        polynomials(later[k + 1])
                    cut(half, like, 3)

            for v, tile in const.items():
                nc.vector.memset(tile[:], float(v)).then_inc(shifts_ready, 1)
            nc.vector.memset(xshift[:], XSHIFT).then_inc(shifts_ready, 1)
            for half in halves(first, first):
                clip(half)
            polynomials(halves(first, first)[0])
            steps(dve, step)

        @block.scalar
        def _(act):
            def evacuate_y(j, par, like):
                act.wait_ge(y_done, j + 1)
                act.wait_ge(consts_ready, j + 1)
                if like >= 0:
                    act.wait_ge(phi_used, l1_over(j - 2))
                nc.scalar.activation(X[0][par][:], y_ps[:], ACT.Relu, bias=consts[:, 2:3],
                                     scale=XSCALE).then_inc(X_ready[0], 1)
                nc.scalar.activation(S[0][par][:], y_ps[:], ACT.Silu, bias=consts[:, 1:2]).then_inc(S_ready[0], 1)

            def evacuate_l1(j, par):
                act.wait_ge(phi_used, l1_over(j))
                nc.scalar.activation(X[1][par][:], l1_ps[par][:], ACT.Relu, bias=xshift[:, 0:1],
                                     scale=XSCALE).then_inc(X_ready[1], 1)
                nc.scalar.activation(S[1][par][:], l1_ps[par][:], ACT.Silu).then_inc(S_ready[1], 1)

            def gelu(j, like):
                act.wait_ge(phi_used, l2_over(j))
                if like >= 1:
                    act.wait_ge(out_stored, 16 * j)
                nc.scalar.activation(act_out[:], l2_ps[:], ACT.Gelu).then_inc(gelu_ready, 1)

            def zigzag(half):
                m, layer, tile, par, rho = half
                f = fold[rho][:]
                if rho == 0:
                    act.wait_ge(X_ready[layer], tile + 1)
                    nc.scalar.activation(f, X[layer][par][:], ACT.Relu, bias=const[10][:], scale=-1.0)\
                        .then_inc(clip0_ready, 1)
                    act.wait_ge(clip0_ready, m + 1)
                else:
                    act.wait_ge(clip_ready, m + 1)
                for k, centre in enumerate((7 if rho else 4, 4, 2)):
                    nc.scalar.activation(f, f, ACT.Abs, bias=const[-centre][:]).then_inc(fold_ready, 1)
                    act.wait_ge(fold_ready, 6 * m + (3 * rho + k + 1))
                if not isinstance(m, int) or m >= 1:
                    act.wait_ge(F_ready, 4 * m + (2 * rho - 2))
                nc.scalar.activation(e_[rho][:], f, ACT.Identity, bias=const[-1][:]).then_inc(zigzag_ready, 1)
                nc.scalar.activation(q_[rho][:], f, ACT.Square, bias=const[-1][:]).then_inc(zigzag_ready, 1)
                nc.scalar.activation(g_[rho][:], f, ACT.Abs, bias=const[-2][:], scale=2.0).then_inc(zigzag_ready, 1)

            def step(i, like):
                now = halves(i, like)
                after = (now + (halves(i + 1, like + 1) if like < last else []))[1:]
                for k in range(len(now)):
                    if k < len(after):
                        zigzag(after[k])
                    if k == 1 and like >= 0 and like + 2 <= last:
                        evacuate_y(i + 2, like % 2, like)
                    if k == 1 and like >= 1:
                        gelu(i - 1, like - 1)
                    if k == min(2, len(now) - 1) and has_l1(like):
                        evacuate_l1(i + 1, (like + 1) % 2)

            act.wait_ge(shifts_ready, 6)
            evacuate_y(0, 0, -1)
            zigzag(halves(first, first)[0])
            evacuate_y(1, 1, -1)
            steps(act, step)
            gelu(last, last)

        @block.tensor
        def _(pe):
            def y(j, par, like):
                pe.wait_ge(x_loaded, 16 * (j + 1))
                pe.wait_ge(rows_loaded, 32 * (j + 1))
                pe.wait_ge(conv_ready, j + 1)
                if not isinstance(j, int) or j > 0:
                    pe.wait_ge(S_ready[0], j)
                src = tile_of(x_ring, j)
                for n in range(TN // MM):
                    nc.tensor.matmul(y_ps[:, n * MM:(n + 1) * MM], conv_t[:], src[:, n * MM:(n + 1) * MM],
                                     start=True, stop=False, skip_group_check=True)
                    for h in range(n * MM // W, (n + 1) * MM // W):
                        ins = nc.tensor.matmul(y_ps[:, h * W:(h + 1) * W], rows[:, par, h, :], inv_w_sb[:],
                                               start=False, stop=((h + 1) % (MM // W) == 0), skip_group_check=True)
                ins.then_inc(y_done, 1)

            def product(dst, layer, f, src):
                for n in range(TN // MM):
                    ins = nc.tensor.matmul(dst[:, n * MM:(n + 1) * MM], kan_w[layer][:, f, :],
                                           src[:, n * MM:(n + 1) * MM], start=(f == 0), stop=(f == NF - 1))
                return ins

            def step(i, like):
                if like >= 0 and like + 2 <= last:
                    y(i + 2, like % 2, like)
                for turn, layer, tile, par, rho in halves(i, like):
                    n = 2 * turn + rho
                    dst = l1_ps[par] if layer == 0 else l2_ps
                    if rho == 0:
                        pe.wait_ge(S_ready[layer], tile + 1)
                        if layer == 1 and like >= 1:
                            pe.wait_ge(gelu_ready, i)
                        product(dst, layer, 0, S[layer][par])
                    for m in range(4):
                        pe.wait_ge(phi_ready, 4 * n + m + 1)
                        ins = product(dst, layer, 1 + 4 * rho + m, phi[rho][m])
                    ins.then_inc(phi_used, 1)

            y(0, 0, -2)
            y(1, 1, -2)
            steps(pe, step)


_INS = ["x", "spec_w1_r", "spec_w1_i", "spec_w2_r", "spec_w2_i", "conv_w", "conv_b", "k1_base", "k1_spline",
        "k1_scaler", "k2_base", "k2_spline", "k2_scaler"]


def kernel(**inputs):
    import numpy as _np
    import concourse.bacc as _bacc
    from concourse import mybir as _mybir
    from concourse.bass_utils import run_bass_kernel_spmd as _run

    nc = _bacc.Bacc("TRN2", target_bir_lowering=False, num_devices=1)
    arrays, args = {}, []
    for name in _INS:
        a = _np.ascontiguousarray(inputs[name if name == "x" else f"L0_conv_{name}"])
        arrays[f"in_{name}_dram"] = a
        args.append(nc.dram_tensor(f"in_{name}_dram", a.shape, _mybir.dt.from_np(a.dtype), kind="ExternalInput").ap())
    for name, a in tables().items():
        arrays[f"{name}_dram"] = a
        args.append(nc.dram_tensor(f"{name}_dram", a.shape, _mybir.dt.from_np(a.dtype), kind="ExternalInput").ap())
    out = nc.dram_tensor("out_0_dram", (B, C, H, W), _mybir.dt.float32, kind="ExternalOutput").ap()
    build(nc, *args, out)
    r = _run(nc, [arrays], core_ids=[0])
    return r.results[0]["out_0_dram"]
```
